# Optimizing a Trainium2 kernel written in Bass

```python
import numpy as np
import jax
import jax.numpy as jnp

def _softmax(x, axis=-1):
    return jax.nn.softmax(x, axis=axis)

def _gelu(x):
    return jax.nn.gelu(x, approximate=True)

def _silu(x):
    return jax.nn.silu(x)

def _sigmoid(x):
    return jax.nn.sigmoid(x)

def _layernorm(x, axis=-1, eps=1e-05):
    m = jnp.mean(x, axis=axis, keepdims=True)
    v = jnp.var(x, axis=axis, keepdims=True)
    return (x - m) / jnp.sqrt(v + eps)

def _scatter_add(tgt, idx, src, axis=0):
    return tgt.at[idx].add(src)

def _segment_sum(src, seg, n):
    return jax.ops.segment_sum(src, seg, n)
kernel_name = 'mk_sandwich_d1_jaxref_r8_ef0829'

def setup_inputs(seed: int=0):
    np.random.seed(seed)
    _w = jnp.asarray

    def _L0_attn_setup():
        import jax, jax.numpy as jnp
        import numpy as np
        B, S, D, DI = (2, 512, 128, 512)

        def _gelu(x):
            return jax.nn.gelu(x, approximate=False)

        def _ln(x, g, b, eps=1e-05):
            mu = jnp.mean(x, axis=-1, keepdims=True)
            var = jnp.mean((x - mu) ** 2, axis=-1, keepdims=True)
            return (x - mu) / jnp.sqrt(var + eps) * g + b

        def _mlp(x, w1, b1, w2, b2):
            return _gelu(x @ w1 + b1) @ w2 + b2
        key = jax.random.key(seed)
        ks = jax.random.split(key, 16)
        s = 0.02

        def W(k, shape):
            return jax.random.normal(k, shape, dtype=jnp.float32) * s
        return {'x': jax.random.normal(ks[0], (B, S, D), dtype=jnp.float32), 'ln_g': jnp.ones((D,), jnp.float32), 'ln_b': jnp.zeros((D,), jnp.float32), 'h1_w1': W(ks[1], (D, DI)), 'h1_b1': jnp.zeros((DI,), jnp.float32), 'h1_w2': W(ks[2], (DI, D)), 'h1_b2': jnp.zeros((D,), jnp.float32), 'h2_w1': W(ks[3], (D, DI)), 'h2_b1': jnp.zeros((DI,), jnp.float32), 'h2_w2': W(ks[4], (DI, D)), 'h2_b2': jnp.zeros((D,), jnp.float32), 'fm_w1': W(ks[5], (D, DI)), 'fm_b1': jnp.zeros((DI,), jnp.float32), 'fm_w2': W(ks[6], (DI, D)), 'fm_b2': jnp.zeros((D,), jnp.float32)}
    _L0_attn_in = _L0_attn_setup()

    def _L0_ffn_setup():
        import jax, jax.numpy as jnp
        import numpy as np
        D_IN, D_HID = (128, 512)

        def _ternary(key, shape):
            return jax.random.randint(key, shape, -1, 2).astype(jnp.float32)

        def _tlin(x, w, s):
            return jnp.einsum('bsi,oi->bso', x, w) * s
        key = jax.random.key(seed)
        ks = jax.random.split(key, 12)
        inv = lambda fan: 1.0 / np.sqrt(fan).astype(np.float32)
        return {'x': jax.random.normal(ks[0], (4, 256, D_IN), dtype=jnp.float32), 'w1_w': _ternary(ks[1], (D_HID, D_IN)), 'w1_s': jax.random.uniform(ks[2], (D_HID,), dtype=jnp.float32) * inv(D_IN), 'w2_w': _ternary(ks[3], (D_HID, D_IN)), 'w2_s': jax.random.uniform(ks[4], (D_HID,), dtype=jnp.float32) * inv(D_IN), 'h1_w': _ternary(ks[5], (D_HID, D_HID)), 'h1_s': jax.random.uniform(ks[6], (D_HID,), dtype=jnp.float32) * inv(D_HID), 'h2_w': _ternary(ks[7], (D_HID, D_HID)), 'h2_s': jax.random.uniform(ks[8], (D_HID,), dtype=jnp.float32) * inv(D_HID), 'w3_w': _ternary(ks[9], (D_IN, D_HID)), 'w3_s': jax.random.uniform(ks[10], (D_IN,), dtype=jnp.float32) * inv(D_HID)}
    _L0_ffn_in = _L0_ffn_setup()
    _d = {'L0_attn_x': _L0_attn_in['x'], 'L0_attn_ln_g': _L0_attn_in['ln_g'], 'L0_attn_ln_b': _L0_attn_in['ln_b'], 'L0_attn_h1_w1': _L0_attn_in['h1_w1'], 'L0_attn_h1_b1': _L0_attn_in['h1_b1'], 'L0_attn_h1_w2': _L0_attn_in['h1_w2'], 'L0_attn_h1_b2': _L0_attn_in['h1_b2'], 'L0_attn_h2_w1': _L0_attn_in['h2_w1'], 'L0_attn_h2_b1': _L0_attn_in['h2_b1'], 'L0_attn_h2_w2': _L0_attn_in['h2_w2'], 'L0_attn_h2_b2': _L0_attn_in['h2_b2'], 'L0_attn_fm_w1': _L0_attn_in['fm_w1'], 'L0_attn_fm_b1': _L0_attn_in['fm_b1'], 'L0_attn_fm_w2': _L0_attn_in['fm_w2'], 'L0_attn_fm_b2': _L0_attn_in['fm_b2'], 'L0_ffn_w1_w': _L0_ffn_in['w1_w'], 'L0_ffn_w1_s': _L0_ffn_in['w1_s'], 'L0_ffn_w2_w': _L0_ffn_in['w2_w'], 'L0_ffn_w2_s': _L0_ffn_in['w2_s'], 'L0_ffn_h1_w': _L0_ffn_in['h1_w'], 'L0_ffn_h1_s': _L0_ffn_in['h1_s'], 'L0_ffn_h2_w': _L0_ffn_in['h2_w'], 'L0_ffn_h2_s': _L0_ffn_in['h2_s'], 'L0_ffn_w3_w': _L0_ffn_in['w3_w'], 'L0_ffn_w3_s': _L0_ffn_in['w3_s']}
    _x0 = _d['L0_attn_x']
    _d['L0_attn_x'] = jax.random.normal(jax.random.fold_in(jax.random.key(seed), 1), (16, 256, 128), dtype=_x0.dtype)
    del _x0
    return _d

def reference(L0_attn_x, L0_attn_ln_g, L0_attn_ln_b, L0_attn_h1_w1, L0_attn_h1_b1, L0_attn_h1_w2, L0_attn_h1_b2, L0_attn_h2_w1, L0_attn_h2_b1, L0_attn_h2_w2, L0_attn_h2_b2, L0_attn_fm_w1, L0_attn_fm_b1, L0_attn_fm_w2, L0_attn_fm_b2, L0_ffn_w1_w, L0_ffn_w1_s, L0_ffn_w2_w, L0_ffn_w2_s, L0_ffn_h1_w, L0_ffn_h1_s, L0_ffn_h2_w, L0_ffn_h2_s, L0_ffn_w3_w, L0_ffn_w3_s):

    def _L0_attn_ref(x, ln_g, ln_b, h1_w1, h1_b1, h1_w2, h1_b2, h2_w1, h2_b1, h2_w2, h2_b2, fm_w1, fm_b1, fm_w2, fm_b2):
        import jax, jax.numpy as jnp
        import numpy as np
        B, S, D, DI = (2, 512, 128, 512)

        def _gelu(x):
            return jax.nn.gelu(x, approximate=False)

        def _ln(x, g, b, eps=1e-05):
            mu = jnp.mean(x, axis=-1, keepdims=True)
            var = jnp.mean((x - mu) ** 2, axis=-1, keepdims=True)
            return (x - mu) / jnp.sqrt(var + eps) * g + b

        def _mlp(x, w1, b1, w2, b2):
            return _gelu(x @ w1 + b1) @ w2 + b2
        n = _ln(x, ln_g, ln_b)
        W1 = _mlp(n, h1_w1, h1_b1, h1_w2, h1_b2)
        W2 = _mlp(n, h2_w1, h2_b1, h2_w2, h2_b2)
        W3 = jnp.einsum('bzn,bsn->bzs', W1, W2)
        W3 = jnp.tril(W3)
        t = jnp.einsum('bzs,bsm->bzm', W3, n)
        t = _ln(_gelu(t), ln_g, ln_b)
        x1 = x + t
        out = x + _mlp(_ln(x1, ln_g, ln_b), fm_w1, fm_b1, fm_w2, fm_b2)
        return out

    def _L0_ffn_ref(x, w1_w, w1_s, w2_w, w2_s, h1_w, h1_s, h2_w, h2_s, w3_w, w3_s):
        import jax, jax.numpy as jnp
        import numpy as np
        D_IN, D_HID = (128, 512)

        def _ternary(key, shape):
            return jax.random.randint(key, shape, -1, 2).astype(jnp.float32)

        def _tlin(x, w, s):
            return jnp.einsum('bsi,oi->bso', x, w) * s
        h = jax.nn.silu(_tlin(x, w1_w, w1_s)) * _tlin(x, w2_w, w2_s)
        h = jax.nn.gelu(_tlin(h, h1_w, h1_s), approximate=False)
        h = jax.nn.gelu(_tlin(h, h2_w, h2_s), approximate=False)
        return _tlin(h, w3_w, w3_s)
    x = L0_attn_x
    x = x + _layernorm(_L0_attn_ref(_layernorm(x, axis=-1), L0_attn_ln_g, L0_attn_ln_b, L0_attn_h1_w1, L0_attn_h1_b1, L0_attn_h1_w2, L0_attn_h1_b2, L0_attn_h2_w1, L0_attn_h2_b1, L0_attn_h2_w2, L0_attn_h2_b2, L0_attn_fm_w1, L0_attn_fm_b1, L0_attn_fm_w2, L0_attn_fm_b2), axis=-1)
    x = x + _layernorm(_L0_ffn_ref(_layernorm(x, axis=-1), L0_ffn_w1_w, L0_ffn_w1_s, L0_ffn_w2_w, L0_ffn_w2_s, L0_ffn_h1_w, L0_ffn_h1_s, L0_ffn_h2_w, L0_ffn_h2_s, L0_ffn_w3_w, L0_ffn_w3_s), axis=-1)
    return x

_drawn_inputs = setup_inputs


def setup_inputs(seed=0):
    import zlib

    import numpy as np

    out = dict(_drawn_inputs(seed))
    spreads = {'L0_attn_ln_g': (1.0, 0.6),
     'L0_attn_ln_b': (0.0, 0.588),
     'L0_attn_h1_b1': (0.0, 0.73),
     'L0_attn_h1_b2': (0.0, 1.034),
     'L0_attn_h2_b1': (0.0, 0.8),
     'L0_attn_h2_b2': (0.0, 0.445),
     'L0_attn_fm_b1': (0.0, 0.666),
     'L0_attn_fm_b2': (0.0, 0.1)}
    factors = {'L0_attn_h1_w1': 3.131, 'L0_attn_h1_w2': 2.873}
    for name, (base, spread) in spreads.items():
        noise = np.random.default_rng([zlib.crc32(name.encode()), seed]).standard_normal(out[name].shape)
        drawn = base * np.exp(spread * noise) if base else spread * noise
        out[name] = jnp.asarray(drawn.astype(out[name].dtype))
    for name, factor in factors.items():
        out[name] = (out[name] * factor).astype(out[name].dtype)
    return out
```

```python
import concourse.bass as bass
from concourse import mybir
from contextlib import ExitStack


class Milestones:

    def __init__(self, sem, names):
        self.sem, self.names, self.at = sem, names.split(), 0

    def step(self, name):
        assert self.names[self.at % len(self.names)] == name, (name, self.names[self.at % len(self.names)])
        self.at += 1
        return 1

    def after(self, name, chunk):
        return chunk * len(self.names) + (self.names.index(name) + 1)


def sandwich_block(nc, x, attn_w, ffn_w, columns, rows, out):
    f32, f32r, i32 = mybir.dt.float32, mybir.dt.float32r, mybir.dt.int32
    ALU, ACT = mybir.AluOpType, mybir.ActivationFunctionType

    P = 128
    B, S, D = x.shape
    TILES = B * S // P
    T = 4
    N = T * P
    CHUNKS = TILES // T
    SEQS = N // S
    DI = attn_w.shape[1] // 6
    J = DI // P
    EPS = 1e-5
    assert D == P and S == 2 * P and J == T

    A_UP = {"h1": 0, "h2": DI, "fm": 4 * DI}
    A_DOWN = {"h1": 2 * DI, "h2": 3 * DI, "fm": 5 * DI}
    F_W1, F_W2, F_W3, F_H1 = 0, DI, 2 * DI, 3 * DI
    F_H2 = F_H1 + J * DI
    C_B1 = {"h1": 0, "h2": J, "fm": 2 * J}
    C_S1, C_S2, C_HS = 3 * J, 4 * J, {"h1": 5 * J, "h2": 6 * J}
    C_B2 = {"h1": 7 * J, "h2": 7 * J + 1}
    C_G, C_B = 7 * J + 2, 7 * J + 3
    R_G, R_B, R_B2, R_S3 = range(4)

    ctx = ExitStack()
    with ctx:
        def sb(name, shape, dt=f32):
            return ctx.enter_context(nc.sbuf_tensor(name, shape, dt))

        def sem(name):
            return ctx.enter_context(nc.semaphore(name))

        X = sb("X", [P, TILES, D])
        Aw = [sb(f"attn_w_{h}", [P, 6 * DI], f32r) for h in ("hi", "lo")]
        Fw = [sb(f"ffn_w_{h}", [P, ffn_w.shape[1]], f32r) for h in ("hi", "lo")]
        raw_a = sb("raw_a", [P, 6 * DI])
        raw_b = sb("raw_b", [P, 3 * DI])
        cols = sb("cols", [P, columns.shape[1]])
        bc = sb("bc", [P, 4, D])
        gate_half = sb("gate_half", [P, J])
        gate_coef = sb("gate_coef", [P, J])
        ident = sb("ident", [P, P])
        mask = sb("mask", [P, 3, P])
        eps = sb("eps", [P, T])
        neg_half = sb("neg_half", [P, T])
        ones = sb("ones", [P, 1])
        lo_sum = sb("lo_sum", [P, 4])
        lo_any = sb("lo_any", [P, 4])
        lo_flag = sb("lo_flag", [1, 1])
        warm = sb("warm", [P, 1])

        N0 = sb("N0", [P, T, D])
        NF = sb("NF", [P, T, D])
        n_tok = [sb(f"n_tok_{h}", [P, T, D], f32r) for h in ("hi", "lo")]
        N0B1 = sb("N0B1", [P, T, D])
        N0B2 = sb("N0B2", [P, T, D])
        X1 = sb("X1", [P, T, D])
        YF = sb("YF", [P, T, D])
        aT = [sb(f"aT_{h}", [P, N], f32r) for h in ("hi", "lo")]
        yT = [sb(f"yT_{h}", [P, N], f32r) for h in ("hi", "lo")]
        WT = {L: [sb(f"{L}T_{h}", [P, N], f32r) for h in ("hi", "lo")] for L in ("h1", "h2")}
        SC = [sb(f"sc_{h}", [P, SEQS, 3, P], f32r) for h in ("hi", "lo")]
        SLOTS = 6
        HA = [sb(f"attn_hidden_{h}", [P, SLOTS, N], f32r) for h in ("hi", "lo")]
        SLOT0 = {"h1": 0, "h2": J, "fm": 2 * J}
        HG = [sb(f"ffn_gate_{h}", [P, J, N], f32r) for h in ("hi", "lo")]
        HF = [sb(f"ffn_h1_{h}", [P, J, N], f32r) for h in ("hi", "lo")]
        TH = sb("TH", [P, N])

        def ln_tiles(name):
            return {"st": sb(f"{name}_st", [P, T, 6]), "mv": sb(f"{name}_mv", [P, T, 2]),
                    "ve": sb(f"{name}_ve", [P, T]), "r": sb(f"{name}_r", [P, T])}

        LN = {k: ln_tiles(f"ln_{k}") for k in ("x", "t", "x1", "o", "y", "f")}
        hv = sb("ln_xx_var", [P, T])
        hd = sb("ln_xx_ve", [P, T])
        hr = sb("ln_xx_r", [P, T])

        pa = [ctx.enter_context(nc.psum_tensor(f"pa{i}", [P, N], f32)) for i in range(4)]
        pf = [ctx.enter_context(nc.psum_tensor(f"pf{i}", [P, N], f32)) for i in range(4)]
        A_ROT = "nT h1u0 h1u1 h1u2 h1u3 h2u0 h2u1 h2u2 h2u3 s0 s1 mT fmu0 fmu1 fmu2 fmu3".split()
        A_LONG = "h1d h2d t fmd".split()
        F_ROT = "yT p0 q0 p1 q1 p2 q2 p3 q3 h1_0 h1_1 h1_2 h1_3 h2_0 h2_1 h2_2 h2_3 w3".split()

        def bank(group):
            if group in A_LONG:
                return pa[3]
            if group in A_ROT:
                return pa[A_ROT.index(group) % 3]
            return pf[F_ROT.index(group) % 4]

        READ_BY = {"nT": "nT_lo", "mT": "mT_lo", "h1d": "h1T_lo", "h2d": "h2T_lo", "t": "t_g", "fmd": "out",
                   "s0": "s_lo0", "s1": "s_lo1", "yT": "yT_lo", "w3": "fo"}
        for L in ("h1", "h2", "fm"):
            READ_BY |= {f"{L}u{j}": f"{L}_lo{j}" for j in range(J)}
        for j in range(J):
            READ_BY |= {f"p{j}": f"u{j}", f"q{j}": f"g_lo{j}", f"h1_{j}": f"h1_lo{j}", f"h2_{j}": f"h2_lo{j}"}

        x_first, x_rest = sem("x_first"), sem("x_rest")
        PIECES = [("a", 0, 2 * DI), ("a", 2 * DI, 4 * DI), ("a", 4 * DI, 6 * DI),
                  ("f", F_W1, F_H1), ("f", F_H1, F_H2), ("f", F_H2, F_H2 + 2 * DI), ("f", F_H2 + 2 * DI, F_H2 + J * DI)]
        w_in = [sem(f"w_in{k}") for k in range(len(PIECES))]
        consts_ready = sem("consts_ready")
        dve_consts = sem("dve_consts")
        split_hi, split_lo_a, split_lo_f = sem("split_hi"), sem("split_lo_a"), sem("split_lo_f")
        lo_summed, lo_tested, lo_counted, lo_flagged = (sem(s) for s in ("lo_summed", "lo_tested", "lo_counted", "lo_flagged"))
        stored = sem("stored")

        lo_names = lambda L: " ".join(f"{L}_lo{j}" for j in range(J))
        head_vector = Milestones(sem("head_vector"), "stats aggr n0 nf n_lo")
        head_pool = Milestones(sem("head_pool"), "ve r vr v0 ve0 r0 n0g n0b1")
        head_scalar = Milestones(sem("head_scalar"), "n_hi")
        attn_tensor = Milestones(sem("attn_tensor"),
            "nT h1u0 h1u1 h1u2 h1u3 h2u0 h1d h2u1 h2u2 h2u3 h2d s0 s1 t mT fmu0 fmu1 fmu2 fmu3 fmd")
        attn_scalar = Milestones(sem("attn_scalar"),
            "nT_hi h1_hi0 h1_g0 h1_hi1 h1_g1 h1_hi2 h1_g2 h1_hi3 h1_g3 h2_hi0 h2_g0 h1T_hi h2_hi1 h2_g1 "
            "h2_hi2 h2_g2 h2_hi3 h2_g3 h2T_hi s_hi0 s_hi1 t mT_hi mT_g fm_hi0 fm_g0 fm_hi1 fm_g1 fm_hi2 fm_g2 fm_hi3 fm_g3")
        attn_vector = Milestones(sem("attn_vector"),
            "nT_lo h1_lo0 h1_lo1 h1_lo2 h1_lo3 h2_lo0 h1T_lo h2_lo1 h2_lo2 h2_lo3 h2T_lo s_mask0 s_lo0 s_mask1 s_lo1 "
            "t_stats t_aggr t_g x1 x1_stats x1_aggr m mT_lo fm_lo0 fm_lo1 fm_lo2 fm_lo3")
        attn_pool = Milestones(sem("attn_pool"), "n0b2 t_ve t_r x1_ve x1_r")
        ffn_tensor = Milestones(sem("ffn_tensor"),
            "yT p0 q0 p1 q1 p2 q2 p3 q3 h1_0 h1_1 h1_2 h1_3 h2_0 h2_1 h2_2 h2_3 w3")
        ffn_scalar = Milestones(sem("ffn_scalar"),
            "yT_hi th0 g_hi0 th1 g_hi1 th2 g_hi2 th3 g_hi3 h1_hi0 h1_g0 h1_hi1 h1_g1 h1_hi2 h1_g2 h1_hi3 h1_g3 "
            "h2_hi0 h2_g0 h2_hi1 h2_g1 h2_hi2 h2_g2 h2_hi3 h2_g3")
        ffn_vector = Milestones(sem("ffn_vector"),
            "out o_stats o_aggr on xo y_stats y_aggr y yT_lo u0 g0 g_lo0 u1 g1 g_lo1 u2 g2 g_lo2 u3 g3 g_lo3 "
            "h1_lo0 h1_lo1 h1_lo2 h1_lo3 h2_lo0 h2_lo1 h2_lo2 h2_lo3 fo f_stats f_aggr fn xf")
        ffn_pool = Milestones(sem("ffn_pool"), "o_ve o_r y_ve y_r f_ve f_r")
        params_in = sem("params_in")
        dve_waited = sem("dve_waited")

        def piece_dst(k, half):
            kind, c0, c1 = PIECES[k]
            return (Aw if kind == "a" else Fw)[half][:, c0:c1]

        def piece_raw(k):
            kind, c0, c1 = PIECES[k]
            if kind == "a":
                return raw_a[:, c0:c1]
            return [raw_b[:, 0:3 * DI], raw_a[:, 0:4 * DI], raw_a[:, 4 * DI:6 * DI], raw_b[:, 0:2 * DI]][k - 3]

        def flat(ap):
            return ap.rearrange("p t d -> p (t d)")

        def row(r):
            return bc[:, r:r + 1, :].broadcast_to([P, T, D])

        block = ctx.enter_context(nc.Block())

        @block.sync
        def _(sp):
            xv = x.rearrange("b (s p) d -> p (b s) d", p=P)
            ov = out.rearrange("b (s p) d -> p (b s) d", p=P)
            sp.dma_start(X[:, 0:T, :], xv[:, 0:T, :]).then_inc(x_first, 16)
            sp.dma_start(piece_raw(0), attn_w[:, 0:2 * DI]).then_inc(w_in[0], 16)
            sp.dma_start(piece_raw(1), attn_w[:, 2 * DI:4 * DI]).then_inc(w_in[1], 16)
            sp.dma_start(piece_raw(2), attn_w[:, 4 * DI:6 * DI]).then_inc(w_in[2], 16)
            sp.dma_start(piece_raw(3), ffn_w[:, F_W1:F_H1]).then_inc(w_in[3], 16)
            sp.dma_start(X[:, T:TILES, :], xv[:, T:TILES, :]).then_inc(x_rest, 16)
            for k in range(4, len(PIECES)):
                sp.wait_ge(split_hi, 4 if k == 6 else 3)
                if k == 6:
                    sp.wait_ge(split_lo_f, 1)
                else:
                    sp.wait_ge(split_lo_a, 3)
                _, c0, c1 = PIECES[k]
                sp.dma_start(piece_raw(k), ffn_w[:, c0:c1]).then_inc(w_in[k], 16)
            for c in range(CHUNKS):
                sp.wait_ge(ffn_vector.sem, ffn_vector.after("xf", c))
                sp.dma_start(ov[:, c * T:(c + 1) * T, :], X[:, c * T:(c + 1) * T, :]).then_inc(stored, 16)
            sp.wait_ge(stored, 16 * CHUNKS)

        @block.gpsimd
        def _(pool):
            pool.dma_start(cols[:, :], columns).then_inc(params_in, 16)
            pool.dma_start(bc[:, :, :], rows.rearrange("(o r) d -> o r d", o=1).broadcast_to([P, 4, D])).then_inc(params_in, 16)
            nc.gpsimd.memset(eps[:, :], EPS)
            nc.gpsimd.memset(neg_half[:, :], -0.5)
            nc.gpsimd.memset(ones[:, :], 1.0)
            nc.gpsimd.memset(ident[:, :], 0.0)
            nc.gpsimd.memset(mask[:, :, :], 1.0).then_inc(consts_ready, 1)
            pool.wait_ge(consts_ready, 1)
            nc.gpsimd.affine_select(out=ident[:, :], in_=ident[:, :], compare_op=ALU.not_equal, fill=1.0,
                                    base=0, pattern=[[-1, P]], channel_multiplier=1).then_inc(consts_ready, 1)
            for k in (0, 2):
                nc.gpsimd.affine_select(out=mask[:, k, :], in_=mask[:, k, :], compare_op=ALU.is_ge, fill=0.0,
                                        base=0, pattern=[[1, P]], channel_multiplier=-1).then_inc(consts_ready, 1)
            pool.wait_ge(params_in, 32)

            def rstd(ms, name, ln, aggr_sem, aggr_value, chunk):
                pool.wait_ge(aggr_sem, aggr_value)
                nc.gpsimd.tensor_tensor(ln["ve"][:, :], ln["mv"][:, :, 1], eps[:, :], ALU.add).then_inc(ms.sem, ms.step(f"{name}ve"))
                pool.wait_ge(ms.sem, ms.after(f"{name}ve", chunk))
                nc.gpsimd.tensor_tensor(ln["r"][:, :], ln["ve"][:, :], neg_half[:, :], ALU.pow).then_inc(ms.sem, ms.step(f"{name}r"))

            def head(c):
                ms = head_pool
                rstd(ms, "", LN["x"], head_vector.sem, head_vector.after("aggr", c), c)
                pool.wait_ge(ms.sem, ms.after("r", c))
                nc.gpsimd.tensor_tensor(hv[:, :], LN["x"]["mv"][:, :, 1], LN["x"]["r"][:, :], ALU.mult).then_inc(ms.sem, ms.step("vr"))
                pool.wait_ge(ms.sem, ms.after("vr", c))
                nc.gpsimd.tensor_tensor(hd[:, :], hv[:, :], LN["x"]["r"][:, :], ALU.mult).then_inc(ms.sem, ms.step("v0"))
                pool.wait_ge(ms.sem, ms.after("v0", c))
                nc.gpsimd.tensor_tensor(hv[:, :], hd[:, :], eps[:, :], ALU.add).then_inc(ms.sem, ms.step("ve0"))
                pool.wait_ge(ms.sem, ms.after("ve0", c))
                nc.gpsimd.tensor_tensor(hr[:, :], hv[:, :], neg_half[:, :], ALU.pow).then_inc(ms.sem, ms.step("r0"))
                pool.wait_ge(head_vector.sem, head_vector.after("n0", c))
                nc.gpsimd.tensor_tensor(NF[:, :, :], N0[:, :, :], row(R_G), ALU.mult).then_inc(ms.sem, ms.step("n0g"))
                nc.gpsimd.tensor_tensor(N0B1[:, :, :], N0[:, :, :], row(R_B), ALU.add).then_inc(ms.sem, ms.step("n0b1"))

            def split(k):
                pool.wait_ge(split_hi, k + 1)
                nc.gpsimd.tensor_tensor(piece_dst(k, 1), piece_raw(k), piece_dst(k, 0).bitcast(f32), ALU.subtract)\
                    .then_inc(split_lo_f, 1)

            def residual_b2(a):
                pool.wait_ge(head_vector.sem, head_vector.after("n0", a))
                if not (isinstance(a, int) and a == 0):
                    pool.wait_ge(ffn_vector.sem, ffn_vector.after("out", a - 1))
                nc.gpsimd.tensor_tensor(N0B2[:, :, :], N0[:, :, :], row(R_B2), ALU.add).then_inc(attn_pool.sem, attn_pool.step("n0b2"))

            def iteration(f, a, h):
                if f is not None:
                    rstd(ffn_pool, "o_", LN["o"], ffn_vector.sem, ffn_vector.after("o_aggr", f), f)
                if a is not None:
                    residual_b2(a)
                if f is not None:
                    rstd(ffn_pool, "y_", LN["y"], ffn_vector.sem, ffn_vector.after("y_aggr", f), f)
                if f is None:
                    for k in range(3, len(PIECES)):
                        split(k)
                if a is not None:
                    rstd(attn_pool, "t_", LN["t"], attn_vector.sem, attn_vector.after("t_aggr", a), a)
                    rstd(attn_pool, "x1_", LN["x1"], attn_vector.sem, attn_vector.after("x1_aggr", a), a)
                if h is not None:
                    head(h)
                if f is not None:
                    rstd(ffn_pool, "f_", LN["f"], ffn_vector.sem, ffn_vector.after("f_aggr", f), f)

            head(0)
            iteration(None, 0, 1)
            with pool.Fori(0, CHUNKS - 2) as i:
                iteration(i, i + 1, i + 2)
            iteration(CHUNKS - 2, CHUNKS - 1, None)
            iteration(CHUNKS - 1, None, None)

        @block.scalar
        def _(act):
            act.wait_ge(consts_ready, 1)
            nc.scalar.activation(warm[:, :], ones[:, :], ACT.Gelu)
            for k in range(3):
                act.wait_ge(w_in[k], 16)
                nc.scalar.activation(piece_dst(k, 0), piece_raw(k), ACT.Copy).then_inc(split_hi, 1)
            act.wait_ge(params_in, 32)

            def head(c):
                if not (isinstance(c, int) and c == 0):
                    act.wait_ge(attn_tensor.sem, attn_tensor.after("t", c - 1))
                act.wait_ge(head_vector.sem, head_vector.after("nf", c))
                nc.scalar.activation(n_tok[0][:, :, :], NF[:, :, :], ACT.Copy).then_inc(head_scalar.sem, head_scalar.step("n_hi"))

            def hi_copy(ms, name, tensor, group, dst, chunk):
                act.wait_ge(tensor.sem, tensor.after(group, chunk))
                nc.scalar.activation(dst, bank(group)[:, :], ACT.Copy).then_inc(ms.sem, ms.step(name))

            def gelu(ms, L, j, tensor, group, dst, chunk, **affine):
                act.wait_ge(tensor.sem, tensor.after(group, chunk))
                nc.scalar.activation(dst, bank(group)[:, :], ACT.Gelu, **affine).then_inc(ms.sem, ms.step(f"{L}_hi{j}"))
                act.wait_ge(ms.sem, ms.after(f"{L}_hi{j}", chunk))
                nc.scalar.activation(bank(group)[:, :], bank(group)[:, :], ACT.Gelu, **affine).then_inc(ms.sem, ms.step(f"{L}_g{j}"))

            def up(L, j, a):
                slot = (SLOT0[L] + j) % SLOTS
                gelu(attn_scalar, L, j, attn_tensor, f"{L}u{j}", HA[0][:, slot, :], a,
                     bias=cols[:, C_B1[L] + j:C_B1[L] + j + 1])

            def down(L, a):
                act.wait_ge(attn_tensor.sem, attn_tensor.after(f"{L}d", a))
                nc.scalar.activation(WT[L][0][:, :], bank(f"{L}d")[:, :], ACT.Identity,
                                     bias=cols[:, C_B2[L]:C_B2[L] + 1]).then_inc(attn_scalar.sem, attn_scalar.step(f"{L}T_hi"))

            def scores(b, a):
                act.wait_ge(attn_vector.sem, attn_vector.after(f"s_mask{b}", a))
                nc.scalar.activation(flat(SC[0][:, b, :, :]), bank(f"s{b}")[:, 0:3 * P], ACT.Copy)\
                    .then_inc(attn_scalar.sem, attn_scalar.step(f"s_hi{b}"))

            def t_gelu(a):
                act.wait_ge(attn_tensor.sem, attn_tensor.after("t", a))
                nc.scalar.activation(bank("t")[:, :], bank("t")[:, :], ACT.Gelu).then_inc(attn_scalar.sem, attn_scalar.step("t"))

            def m_transposed(a):
                act.wait_ge(attn_tensor.sem, attn_tensor.after("mT", a))
                g, b = cols[:, C_G:C_G + 1], cols[:, C_B:C_B + 1]
                nc.scalar.activation(aT[0][:, :], bank("mT")[:, :], ACT.Identity, scale=g, bias=b)\
                    .then_inc(attn_scalar.sem, attn_scalar.step("mT_hi"))
                act.wait_ge(attn_scalar.sem, attn_scalar.after("mT_hi", a))
                nc.scalar.activation(bank("mT")[:, :], bank("mT")[:, :], ACT.Identity, scale=g, bias=b)\
                    .then_inc(attn_scalar.sem, attn_scalar.step("mT_g"))

            def tanh(j, f):
                if j:
                    act.wait_ge(ffn_vector.sem, ffn_vector.after(f"g{j - 1}", f))
                act.wait_ge(ffn_tensor.sem, ffn_tensor.after(f"p{j}", f))
                nc.scalar.activation(TH[:, :], bank(f"p{j}")[:, :], ACT.Tanh, scale=gate_half[:, j:j + 1])\
                    .then_inc(ffn_scalar.sem, ffn_scalar.step(f"th{j}"))

            def gate_hi(j, f):
                act.wait_ge(ffn_vector.sem, ffn_vector.after(f"g{j}", f))
                nc.scalar.activation(HG[0][:, j, :], bank(f"q{j}")[:, :], ACT.Copy)\
                    .then_inc(ffn_scalar.sem, ffn_scalar.step(f"g_hi{j}"))

            def layer(L, j, f):
                dst = HF if L == "h1" else HG
                gelu(ffn_scalar, L, j, ffn_tensor, f"{L}_{j}", dst[0][:, j, :], f,
                     scale=cols[:, C_HS[L] + j:C_HS[L] + j + 1])

            def iteration(f, a, h):
                if a is not None:
                    hi_copy(attn_scalar, "nT_hi", attn_tensor, "nT", aT[0][:, :], a)
                    for j in range(J):
                        up("h1", j, a)
                    up("h2", 0, a)
                    down("h1", a)
                    up("h2", 1, a)
                    up("h2", 2, a)
                    up("h2", 3, a)
                if f is None:
                    for k in range(3, len(PIECES)):
                        act.wait_ge(w_in[k], 16)
                        nc.scalar.activation(piece_dst(k, 0), piece_raw(k), ACT.Copy).then_inc(split_hi, 1)
                if f is not None:
                    hi_copy(ffn_scalar, "yT_hi", ffn_tensor, "yT", yT[0][:, :], f)
                    tanh(0, f)
                if a is not None:
                    down("h2", a)
                if f is not None:
                    for j in range(1, J):
                        gate_hi(j - 1, f)
                        tanh(j, f)
                if a is not None:
                    scores(0, a)
                if f is not None:
                    gate_hi(J - 1, f)
                if a is not None:
                    scores(1, a)
                if f is not None:
                    layer("h1", 0, f)
                    layer("h1", 1, f)
                if a is not None:
                    t_gelu(a)
                if f is None:
                    for k in range(3, len(PIECES)):
                        act.wait_ge(split_lo_f, len(PIECES) - 3)
                        if k == len(PIECES) - 1:
                            act.wait_ge(lo_summed, k - 3)
                        nc.scalar.activation(piece_raw(k), piece_dst(k, 1).bitcast(f32), ACT.Abs,
                                             accum_out=lo_sum[:, k - 3:k - 2]).then_inc(lo_summed, 1)
                if f is not None:
                    layer("h1", 2, f)
                    layer("h1", 3, f)
                    layer("h2", 0, f)
                    layer("h2", 1, f)
                if h is not None:
                    head(h)
                if f is not None:
                    layer("h2", 2, f)
                    layer("h2", 3, f)
                if a is not None:
                    m_transposed(a)
                    for j in range(J):
                        up("fm", j, a)

            head(0)
            iteration(None, 0, 1)
            with act.Fori(0, CHUNKS - 2) as i:
                iteration(i, i + 1, i + 2)
            iteration(CHUNKS - 2, CHUNKS - 1, None)
            iteration(CHUNKS - 1, None, None)

        @block.vector
        def _(dve):
            def alone():
                nc.vector.sem_inc(dve_waited, 1)

            def stats(ms, name, src, ln, chunk):
                for t in range(T):
                    last = nc.vector.bn_stats(ln["st"][:, t, :], src(t))
                last.then_inc(ms.sem, ms.step(f"{name}stats"))
                dve.wait_ge(ms.sem, ms.after(f"{name}stats", chunk))
                alone()
                for t in range(T):
                    last = nc.vector.bn_aggr(ln["mv"][:, t, :], ln["st"][:, t, :])
                last.then_inc(ms.sem, ms.step(f"{name}aggr"))

            def normalise(ms, name, dst, src, ln):
                for t in range(T):
                    last = nc.vector.tensor_scalar(dst(t), src(t), ln["mv"][:, t, 0:1], ln["r"][:, t:t + 1],
                                                   ALU.subtract, ALU.mult)
                last.then_inc(ms.sem, ms.step(name))

            def x_tile(c):
                return lambda t: X[:, c * T + t, :]

            def tile_of(buf):
                return lambda t: buf[:, t, :]

            def chunk_of_x(c):
                return X[:, bass.ds(c * T, T), :]

            def low(ms, name, dst, whole, high):
                nc.vector.tensor_tensor(dst, whole, high.bitcast(f32), ALU.subtract).then_inc(ms.sem, ms.step(name))

            def head(c):
                ms = head_vector
                first = isinstance(c, int) and c == 0
                if not first:
                    dve.wait_ge(head_pool.sem, head_pool.after("n0b1", c - 1))
                    alone()
                stats(ms, "", x_tile(c), LN["x"], c)
                if not first:
                    dve.wait_ge(attn_pool.sem, attn_pool.after("n0b2", c - 1))
                dve.wait_ge(head_pool.sem, head_pool.after("r", c))
                normalise(ms, "n0", tile_of(N0), x_tile(c), LN["x"])
                dve.wait_ge(head_pool.sem, head_pool.after("n0g", c))
                for t in range(T):
                    last = nc.vector.scalar_tensor_tensor(NF[:, t, :], NF[:, t, :], hr[:, t:t + 1], bc[:, R_B, :],
                                                          ALU.mult, ALU.add)
                last.then_inc(ms.sem, ms.step("nf"))
                dve.wait_ge(head_scalar.sem, head_scalar.after("n_hi", c))
                dve.wait_ge(ms.sem, ms.after("nf", c))
                low(ms, "n_lo", n_tok[1][:, :, :], NF[:, :, :], n_tok[0][:, :, :])

            def attn_low(name, scalar_step, dst, group, high, a):
                dve.wait_ge(attn_scalar.sem, attn_scalar.after(scalar_step, a))
                low(attn_vector, name, dst, bank(group)[:, :], high)

            def up_low(L, j, a):
                slot = (SLOT0[L] + j) % SLOTS
                attn_low(f"{L}_lo{j}", f"{L}_g{j}", HA[1][:, slot, :], f"{L}u{j}", HA[0][:, slot, :], a)

            def down_low(L, a):
                dve.wait_ge(attn_scalar.sem, attn_scalar.after(f"{L}T_hi", a))
                nc.vector.scalar_tensor_tensor(WT[L][1][:, :], bank(f"{L}d")[:, :], cols[:, C_B2[L]:C_B2[L] + 1],
                                               WT[L][0][:, :].bitcast(f32), ALU.add, ALU.subtract)\
                    .then_inc(attn_vector.sem, attn_vector.step(f"{L}T_lo"))

            def score_mask(b, a):
                dve.wait_ge(attn_tensor.sem, attn_tensor.after(f"s{b}", a))
                nc.vector.tensor_tensor(bank(f"s{b}")[:, 0:3 * P], bank(f"s{b}")[:, 0:3 * P], flat(mask[:, :, :]), ALU.mult)\
                    .then_inc(attn_vector.sem, attn_vector.step(f"s_mask{b}"))

            def score_low(b, a):
                dve.wait_ge(attn_scalar.sem, attn_scalar.after(f"s_hi{b}", a))
                low(attn_vector, f"s_lo{b}", flat(SC[1][:, b, :, :]), bank(f"s{b}")[:, 0:3 * P], flat(SC[0][:, b, :, :]))

            def t_norm(a):
                ms = attn_vector
                tb = bank("t")[:, :].rearrange("p (t d) -> p t d", t=T)
                dve.wait_ge(attn_scalar.sem, attn_scalar.after("t", a))
                alone()
                stats(ms, "t_", tile_of(tb), LN["t"], a)
                dve.wait_ge(ms.sem, ms.after("t_aggr", a))
                for t in range(T):
                    last = nc.vector.scalar_tensor_tensor(X1[:, t, :], tb[:, t, :], LN["t"]["mv"][:, t, 0:1],
                                                          bc[:, R_G, :], ALU.subtract, ALU.mult)
                last.then_inc(ms.sem, ms.step("t_g"))

            def x1_sum(a):
                ms = attn_vector
                dve.wait_ge(head_pool.sem, head_pool.after("n0b1", a))
                dve.wait_ge(attn_pool.sem, attn_pool.after("t_r", a))
                dve.wait_ge(ms.sem, ms.after("t_g", a))
                for t in range(T):
                    last = nc.vector.scalar_tensor_tensor(X1[:, t, :], X1[:, t, :], LN["t"]["r"][:, t:t + 1],
                                                          N0B1[:, t, :], ALU.mult, ALU.add)
                last.then_inc(ms.sem, ms.step("x1"))
                dve.wait_ge(ms.sem, ms.after("x1", a))
                alone()
                stats(ms, "x1_", tile_of(X1), LN["x1"], a)

            def m_norm(a):
                dve.wait_ge(attn_pool.sem, attn_pool.after("x1_r", a))
                normalise(attn_vector, "m", tile_of(X1), tile_of(X1), LN["x1"])

            def branch_out(f):
                ms = ffn_vector
                dve.wait_ge(attn_pool.sem, attn_pool.after("n0b2", f))
                dve.wait_ge(attn_tensor.sem, attn_tensor.after("fmd", f))
                nc.vector.tensor_tensor(flat(X1[:, :, :]), bank("fmd")[:, :], flat(N0B2[:, :, :]), ALU.add)\
                    .then_inc(ms.sem, ms.step("out"))
                dve.wait_ge(ms.sem, ms.after("out", f))
                alone()
                stats(ms, "o_", tile_of(X1), LN["o"], f)

            def x_after_attention(f):
                ms = ffn_vector
                dve.wait_ge(ffn_pool.sem, ffn_pool.after("o_r", f))
                normalise(ms, "on", tile_of(X1), tile_of(X1), LN["o"])
                dve.wait_ge(ms.sem, ms.after("on", f))
                nc.vector.tensor_tensor(chunk_of_x(f), chunk_of_x(f), X1[:, :, :], ALU.add).then_inc(ms.sem, ms.step("xo"))
                dve.wait_ge(ms.sem, ms.after("xo", f))
                alone()
                stats(ms, "y_", x_tile(f), LN["y"], f)

            def y_norm(f):
                dve.wait_ge(ffn_pool.sem, ffn_pool.after("y_r", f))
                normalise(ffn_vector, "y", tile_of(YF), x_tile(f), LN["y"])

            def gate(j, f):
                ms = ffn_vector
                dve.wait_ge(ffn_tensor.sem, ffn_tensor.after(f"q{j}", f))
                dve.wait_ge(ffn_scalar.sem, ffn_scalar.after(f"th{j}", f))
                nc.vector.scalar_tensor_tensor(TH[:, :], TH[:, :], 1.0, bank(f"p{j}")[:, :], ALU.add, ALU.mult)\
                    .then_inc(ms.sem, ms.step(f"u{j}"))
                dve.wait_ge(ms.sem, ms.after(f"u{j}", f))
                nc.vector.scalar_tensor_tensor(bank(f"q{j}")[:, :], TH[:, :], gate_coef[:, j:j + 1], bank(f"q{j}")[:, :],
                                               ALU.mult, ALU.mult).then_inc(ms.sem, ms.step(f"g{j}"))

            def gate_low(j, f):
                dve.wait_ge(ffn_scalar.sem, ffn_scalar.after(f"g_hi{j}", f))
                low(ffn_vector, f"g_lo{j}", HG[1][:, j, :], bank(f"q{j}")[:, :], HG[0][:, j, :])

            def layer_low(L, j, f):
                buf = HF if L == "h1" else HG
                dve.wait_ge(ffn_scalar.sem, ffn_scalar.after(f"{L}_g{j}", f))
                low(ffn_vector, f"{L}_lo{j}", buf[1][:, j, :], bank(f"{L}_{j}")[:, :], buf[0][:, j, :])

            def ffn_scale(f):
                ms = ffn_vector
                dve.wait_ge(ffn_tensor.sem, ffn_tensor.after("w3", f))
                nc.vector.tensor_tensor(YF[:, :, :], bank("w3")[:, :].rearrange("p (t d) -> p t d", t=T), row(R_S3), ALU.mult)\
                    .then_inc(ms.sem, ms.step("fo"))
                dve.wait_ge(ms.sem, ms.after("fo", f))
                alone()
                stats(ms, "f_", tile_of(YF), LN["f"], f)

            def ffn_out(f):
                ms = ffn_vector
                dve.wait_ge(ffn_pool.sem, ffn_pool.after("f_r", f))
                normalise(ms, "fn", tile_of(YF), tile_of(YF), LN["f"])
                dve.wait_ge(ms.sem, ms.after("fn", f))
                nc.vector.tensor_tensor(chunk_of_x(f), chunk_of_x(f), YF[:, :, :], ALU.add).then_inc(ms.sem, ms.step("xf"))

            def iteration(f, a, h):
                if f is not None:
                    branch_out(f)
                if a is not None:
                    attn_low("nT_lo", "nT_hi", aT[1][:, :], "nT", aT[0][:, :], a)
                if f is not None:
                    x_after_attention(f)
                if a is not None:
                    up_low("h1", 0, a)
                    up_low("h1", 1, a)
                if f is not None:
                    y_norm(f)
                if a is not None:
                    up_low("h1", 2, a)
                    up_low("h1", 3, a)
                    up_low("h2", 0, a)
                    down_low("h1", a)
                    for j in range(1, J):
                        up_low("h2", j, a)
                if f is not None:
                    dve.wait_ge(ffn_scalar.sem, ffn_scalar.after("yT_hi", f))
                    low(ffn_vector, "yT_lo", yT[1][:, :], bank("yT")[:, :], yT[0][:, :])
                    gate(0, f)
                if a is not None:
                    down_low("h2", a)
                if f is not None:
                    gate_low(0, f)
                    gate(1, f)
                    gate_low(1, f)
                    gate(2, f)
                if a is not None:
                    score_mask(0, a)
                if f is not None:
                    gate_low(2, f)
                    gate(3, f)
                if a is not None:
                    score_low(0, a)
                    score_mask(1, a)
                if f is not None:
                    gate_low(3, f)
                if a is not None:
                    score_low(1, a)
                if f is not None:
                    layer_low("h1", 0, f)
                    layer_low("h1", 1, f)
                if a is not None:
                    t_norm(a)
                if f is not None:
                    layer_low("h1", 2, f)
                if a is not None:
                    x1_sum(a)
                if f is not None:
                    layer_low("h1", 3, f)
                    layer_low("h2", 0, f)
                if a is not None:
                    m_norm(a)
                if f is not None:
                    layer_low("h2", 1, f)
                if h is not None:
                    head(h)
                if f is not None:
                    layer_low("h2", 2, f)
                    layer_low("h2", 3, f)
                if a is not None:
                    attn_low("mT_lo", "mT_g", aT[1][:, :], "mT", aT[0][:, :], a)
                    for j in range(J):
                        up_low("fm", j, a)
                if f is not None:
                    ffn_scale(f)
                    ffn_out(f)

            dve.wait_ge(params_in, 32)
            nc.vector.tensor_scalar(gate_half[:, :], cols[:, C_S1:C_S1 + J], 0.5, None, ALU.mult).then_inc(dve_consts, 1)
            dve.wait_ge(dve_consts, 1)
            nc.vector.tensor_tensor(gate_coef[:, :], gate_half[:, :], cols[:, C_S2:C_S2 + J], ALU.mult).then_inc(dve_consts, 1)
            dve.wait_ge(dve_consts, 2)
            dve.wait_ge(consts_ready, 4)
            dve.wait_ge(x_first, 16)
            alone()
            head(0)
            for k in range(3):
                dve.wait_ge(split_hi, k + 1)
                nc.vector.tensor_tensor(piece_dst(k, 1), piece_raw(k), piece_dst(k, 0).bitcast(f32), ALU.subtract)\
                    .then_inc(split_lo_a, 1)
            dve.wait_ge(x_rest, 16)
            iteration(None, 0, 1)
            dve.wait_ge(lo_summed, 4)
            nc.vector.tensor_scalar(lo_any[:, :], lo_sum[:, :], 0.0, None, ALU.not_equal).then_inc(lo_tested, 1)
            dve.wait_ge(lo_counted, 1)
            nc.vector.tensor_reduce(lo_flag[0:1, 0:1], pf[0][0:1, 0:4], mybir.AxisListType.X, ALU.add).then_inc(lo_flagged, 1)
            with dve.Fori(0, CHUNKS - 2) as i:
                iteration(i, i + 1, i + 2)
            iteration(CHUNKS - 2, CHUNKS - 1, None)
            iteration(CHUNKS - 1, None, None)

        @block.tensor
        def _(pe):
            def free(ms, group, chunk):
                pe.wait_ge(ms.sem, ms.after(READ_BY[group], chunk))

            def bank_free(group, chunk):
                if group in A_LONG:
                    k = A_LONG.index(group)
                    if k:
                        free(attn_vector, A_LONG[k - 1], chunk)
                    elif not (isinstance(chunk, int) and chunk == 0):
                        free(ffn_vector, "fmd", chunk - 1)
                elif group in A_ROT:
                    k = A_ROT.index(group)
                    if k >= 3:
                        free(attn_vector, A_ROT[k - 3], chunk)
                    elif not (isinstance(chunk, int) and chunk == 0):
                        users = [g for n, g in enumerate(A_ROT) if n % 3 == k]
                        free(attn_vector, users[-1], chunk - 1)
                else:
                    k = F_ROT.index(group)
                    if k >= 4:
                        free(ffn_vector, F_ROT[k - 4], chunk)

            def transposes(ms, group, src, chunk):
                bank_free(group, chunk)
                for t in range(T):
                    last = nc.tensor.transpose(bank(group)[:, t * P:(t + 1) * P], src[:, t, :], ident[:, :])
                last.then_inc(ms.sem, ms.step(group))

            def up(L, j, a):
                g = f"{L}u{j}"
                bank_free(g, a)
                if j == 0:
                    pe.wait_ge(attn_scalar.sem, attn_scalar.after("mT_hi" if L == "fm" else "nT_hi", a))
                w = slice(A_UP[L] + j * P, A_UP[L] + (j + 1) * P)
                nc.tensor.matmul(bank(g)[:, :], Aw[1][:, w], aT[0][:, :], start=True, stop=False)
                nc.tensor.matmul(bank(g)[:, :], Aw[0][:, w], aT[0][:, :], start=False, stop=False)
                if j == 0:
                    pe.wait_ge(attn_vector.sem, attn_vector.after("mT_lo" if L == "fm" else "nT_lo", a))
                nc.tensor.matmul(bank(g)[:, :], Aw[0][:, w], aT[1][:, :], start=False, stop=True)\
                    .then_inc(attn_tensor.sem, attn_tensor.step(g))

            def down(L, k, a):
                g = f"{L}d"
                if k == 0:
                    bank_free(g, a)
                w = slice(A_DOWN[L] + k * P, A_DOWN[L] + (k + 1) * P)
                slot = (SLOT0[L] + k) % SLOTS
                pe.wait_ge(attn_vector.sem, attn_vector.after(f"{L}_lo{k}", a))
                nc.tensor.matmul(bank(g)[:, :], Aw[1][:, w], HA[0][:, slot, :], start=(k == 0), stop=False)
                nc.tensor.matmul(bank(g)[:, :], Aw[0][:, w], HA[0][:, slot, :], start=False, stop=False)
                last = nc.tensor.matmul(bank(g)[:, :], Aw[0][:, w], HA[1][:, slot, :], start=False, stop=(k == J - 1))
                if k == J - 1:
                    last.then_inc(attn_tensor.sem, attn_tensor.step(g))

            def scores(b, a):
                g = f"s{b}"
                bank_free(g, a)
                if b == 0:
                    pe.wait_ge(attn_vector.sem, attn_vector.after("h2T_lo", a))
                o = b * S
                W1, W2 = WT["h1"], WT["h2"]
                for c0, s0, z0, z1 in ((0, o, o, o + S), (2 * P, o + P, o + P, o + S)):
                    for n, (x2, x1) in enumerate(((1, 0), (0, 0), (0, 1))):
                        last = nc.tensor.matmul(bank(g)[:, c0:c0 + z1 - z0], W2[x2][:, s0:s0 + P], W1[x1][:, z0:z1],
                                                start=(n == 0), stop=(n == 2))
                last.then_inc(attn_tensor.sem, attn_tensor.step(g))

            def t_product(a):
                bank_free("t", a)
                pe.wait_ge(attn_vector.sem, attn_vector.after("s_lo1", a))
                for b in range(SEQS):
                    for z, blocks in ((0, ((0, 0),)), (1, ((1, 0), (2, 1)))):
                        c0 = (2 * b + z) * P
                        steps = [(k, s, i, j) for k, s in blocks for i, j in ((1, 0), (0, 0), (0, 1))]
                        for n, (k, s, i, j) in enumerate(steps):
                            last = nc.tensor.matmul(bank("t")[:, c0:c0 + P], SC[i][:, b, k, :], n_tok[j][:, 2 * b + s, :],
                                                    start=(n == 0), stop=(n == len(steps) - 1))
                last.then_inc(attn_tensor.sem, attn_tensor.step("t"))

            def fm_down(a):
                bank_free("fmd", a)
                pe.wait_ge(attn_vector.sem, attn_vector.after(f"fm_lo{J - 1}", a))
                for t in range(T):
                    for k in range(J):
                        w = slice(A_DOWN["fm"] + k * P, A_DOWN["fm"] + (k + 1) * P)
                        slot = (SLOT0["fm"] + k) % SLOTS
                        for n, (i, j) in enumerate(((0, 1), (0, 0), (1, 0))):
                            last = nc.tensor.matmul(bank("fmd")[:, t * P:(t + 1) * P], HA[i][:, slot, t * P:(t + 1) * P],
                                                    Aw[j][:, w], start=(k == 0 and n == 0), stop=(k == J - 1 and n == 2))
                last.then_inc(attn_tensor.sem, attn_tensor.step("fmd"))

            def gate(j, f, lo_pass):
                if j == 0:
                    pe.wait_ge(ffn_vector.sem, ffn_vector.after("yT_lo", f))
                for g, base in ((f"p{j}", F_W1), (f"q{j}", F_W2)):
                    bank_free(g, f)
                    w = slice(base + j * P, base + (j + 1) * P)
                    nc.tensor.matmul(bank(g)[:, :], Fw[0][:, w], yT[1][:, :], start=True, stop=False)
                    if lo_pass:
                        nc.tensor.matmul(bank(g)[:, :], Fw[1][:, w], yT[0][:, :], start=False, stop=False)
                    nc.tensor.matmul(bank(g)[:, :], Fw[0][:, w], yT[0][:, :], start=False, stop=True)\
                        .then_inc(ffn_tensor.sem, ffn_tensor.step(g))

            def layer(L, j, f, lo_pass):
                g = f"{L}_{j}"
                src, base = (HG, F_H1) if L == "h1" else (HF, F_H2)
                bank_free(g, f)
                for k in range(J):
                    if j == 0:
                        pe.wait_ge(ffn_vector.sem, ffn_vector.after(f"g_lo{k}" if L == "h1" else f"h1_lo{k}", f))
                    w = slice(base + k * DI + j * P, base + k * DI + (j + 1) * P)
                    nc.tensor.matmul(bank(g)[:, :], Fw[0][:, w], src[1][:, k, :], start=(k == 0), stop=False)
                    if lo_pass:
                        nc.tensor.matmul(bank(g)[:, :], Fw[1][:, w], src[0][:, k, :], start=False, stop=False)
                    last = nc.tensor.matmul(bank(g)[:, :], Fw[0][:, w], src[0][:, k, :], start=False, stop=(k == J - 1))
                last.then_inc(ffn_tensor.sem, ffn_tensor.step(g))

            def w3(f, lo_pass):
                bank_free("w3", f)
                pe.wait_ge(ffn_vector.sem, ffn_vector.after(f"h2_lo{J - 1}", f))
                halves = ((1, 0), (0, 0), (0, 1)) if lo_pass else ((1, 0), (0, 0))
                for t in range(T):
                    for k in range(J):
                        w = slice(F_W3 + k * P, F_W3 + (k + 1) * P)
                        for n, (i, j) in enumerate(halves):
                            last = nc.tensor.matmul(bank("w3")[:, t * P:(t + 1) * P], HG[i][:, k, t * P:(t + 1) * P],
                                                    Fw[j][:, w], start=(k == 0 and n == 0),
                                                    stop=(k == J - 1 and n == len(halves) - 1))
                last.then_inc(ffn_tensor.sem, ffn_tensor.step("w3"))

            def iteration(f, a, lo_pass):
                if a is not None:
                    pe.wait_ge(head_vector.sem, head_vector.after("n_lo", a))
                    transposes(attn_tensor, "nT", NF, a)
                    if f is None:
                        pe.wait_ge(split_lo_a, 2)
                    up("h1", 0, a)
                    up("h1", 1, a)
                    up("h1", 2, a)
                    down("h1", 0, a)
                    up("h1", 3, a)
                    down("h1", 1, a)
                    up("h2", 0, a)
                    down("h1", 2, a)
                    down("h1", 3, a)
                    up("h2", 1, a)
                    up("h2", 2, a)
                    up("h2", 3, a)
                    down("h2", 0, a)
                    down("h2", 1, a)
                if f is not None:
                    pe.wait_ge(ffn_vector.sem, ffn_vector.after("y", f))
                    transposes(ffn_tensor, "yT", YF, f)
                if a is not None:
                    down("h2", 2, a)
                    down("h2", 3, a)
                if f is not None:
                    gate(0, f, lo_pass)
                    gate(1, f, lo_pass)
                if a is not None:
                    scores(0, a)
                if f is not None:
                    gate(2, f, lo_pass)
                if a is not None:
                    scores(1, a)
                if f is not None:
                    gate(3, f, lo_pass)
                    layer("h1", 0, f, lo_pass)
                    layer("h1", 1, f, lo_pass)
                if a is not None:
                    t_product(a)
                if f is not None:
                    layer("h1", 2, f, lo_pass)
                    layer("h1", 3, f, lo_pass)
                    for j in range(J):
                        layer("h2", j, f, lo_pass)
                if a is not None:
                    if f is None:
                        pe.wait_ge(split_lo_a, 3)
                    pe.wait_ge(attn_vector.sem, attn_vector.after("m", a))
                    transposes(attn_tensor, "mT", X1, a)
                    for j in range(J):
                        up("fm", j, a)
                if f is not None:
                    w3(f, lo_pass)
                if a is not None:
                    fm_down(a)

            pe.wait_ge(consts_ready, 4)
            iteration(None, 0, False)
            pe.wait_ge(split_lo_f, 4)
            pe.wait_ge(lo_tested, 1)
            nc.tensor.matmul(pf[0][0:1, 0:4], ones[:, :], lo_any[:, :], start=True, stop=True).then_inc(lo_counted, 1)
            pe.wait_ge(lo_flagged, 1)
            any_lo = pe.value_load(lo_flag[0:1, 0:1].bitcast(i32))

            def stream(lo_pass):
                with pe.Fori(0, CHUNKS - 2) as i:
                    iteration(i, i + 1, lo_pass)
                iteration(CHUNKS - 2, CHUNKS - 1, lo_pass)
                iteration(CHUNKS - 1, None, lo_pass)

            with pe.If(any_lo > 0):
                stream(True)
            with pe.Else():
                stream(False)


def kernel(**inputs):
    import numpy as _np
    import concourse.bacc as _bacc
    from concourse import mybir as _mybir
    from concourse.bass_utils import run_bass_kernel_spmd as _run

    g = {k: _np.asarray(v) for k, v in inputs.items()}

    def k_tiles(w):
        return w.reshape(-1, 128, w.shape[1]).transpose(1, 0, 2).reshape(128, -1)

    def by_partition(v):
        return v.reshape(-1, 128).T

    a, f = "L0_attn_", "L0_ffn_"
    arrays = {
        "x": g[a + "x"],
        "attn_w": _np.concatenate([g[a + "h1_w1"], g[a + "h2_w1"], k_tiles(g[a + "h1_w2"]), k_tiles(g[a + "h2_w2"]),
                                   g[a + "fm_w1"], k_tiles(g[a + "fm_w2"])], axis=1),
        "ffn_w": _np.concatenate([k_tiles(g[f + n].T) for n in ("w1_w", "w2_w", "w3_w", "h1_w", "h2_w")], axis=1),
        "columns": _np.concatenate([by_partition(g[n]) for n in (
            a + "h1_b1", a + "h2_b1", a + "fm_b1", f + "w1_s", f + "w2_s", f + "h1_s", f + "h2_s",
            a + "h1_b2", a + "h2_b2", a + "ln_g", a + "ln_b")], axis=1),
        "rows": _np.stack([g[a + "ln_g"], g[a + "ln_b"], g[a + "fm_b2"], g[f + "w3_s"]]),
    }
    nc = _bacc.Bacc("TRN2", target_bir_lowering=False, num_devices=1)
    args = []
    for name in arrays:
        arrays[name] = _np.ascontiguousarray(arrays[name])
        args.append(nc.dram_tensor(name, arrays[name].shape, _mybir.dt.from_np(arrays[name].dtype), kind="ExternalInput").ap())
    out = nc.dram_tensor("out", g[a + "x"].shape, _mybir.dt.from_np(g[a + "x"].dtype), kind="ExternalOutput").ap()
    sandwich_block(nc, *args, out)
    r = _run(nc, [arrays], core_ids=[0])
    return r.results[0]["out"]
```

```python
import concourse.bass as bass
from concourse import mybir
from contextlib import ExitStack


class Milestones:

    def __init__(self, sem, names, base=0):
        self.sem, self.names, self.at, self.base = sem, names.split(), 0, base

    def step(self, name):
        assert self.names[self.at % len(self.names)] == name, (name, self.names[self.at % len(self.names)])
        self.at += 1
        return 1

    def after(self, name, chunk):
        return chunk * len(self.names) + (self.names.index(name) + 1 + self.base)


def sandwich_block(nc, x, attn_w, ffn_w, columns, rows, out):
    f32, f32r, i32 = mybir.dt.float32, mybir.dt.float32r, mybir.dt.int32
    ALU, ACT = mybir.AluOpType, mybir.ActivationFunctionType

    P = 128
    B, S, D = x.shape
    TILES = B * S // P
    T = 4
    N = T * P
    CHUNKS = TILES // T
    SEQS = N // S
    DI = attn_w.shape[1] // 6
    J = DI // P
    EPS = 1e-5
    assert D == P and S == 2 * P and J == T

    A_UP = {"h1": 0, "h2": DI, "fm": 4 * DI}
    A_DOWN = {"h1": 2 * DI, "h2": 3 * DI, "fm": 5 * DI}
    F_W1, F_W2, F_W3, F_H1 = 0, DI, 2 * DI, 3 * DI
    F_H2 = F_H1 + J * DI
    C_B1 = {"h1": 0, "h2": J, "fm": 2 * J}
    C_S1, C_S2, C_HS = 3 * J, 4 * J, {"h1": 5 * J, "h2": 6 * J}
    C_B2 = {"h1": 7 * J, "h2": 7 * J + 1}
    C_G, C_B, C_S3 = 7 * J + 2, 7 * J + 3, 7 * J + 4
    R_G, R_B, R_B2 = range(3)

    ctx = ExitStack()
    with ctx:
        def sb(name, shape, dt=f32):
            return ctx.enter_context(nc.sbuf_tensor(name, shape, dt))

        def sem(name):
            return ctx.enter_context(nc.semaphore(name))

        X = sb("X", [P, TILES, D])
        Aw = [sb(f"attn_w_{h}", [P, 6 * DI], f32r) for h in ("hi", "lo")]
        Fw = [sb(f"ffn_w_{h}", [P, ffn_w.shape[1]], f32r) for h in ("hi", "lo")]
        raw_a = sb("raw_a", [P, 6 * DI])
        raw_b = sb("raw_b", [P, 3 * DI])
        cols = sb("cols", [P, columns.shape[1]])
        bc = sb("bc", [P, 3, D])
        gate_half = sb("gate_half", [P, J])
        gate_coef = sb("gate_coef", [P, J])
        ident = sb("ident", [P, P])
        mask = sb("mask", [P, 2, P])
        eps = sb("eps", [P, T])
        neg_half = sb("neg_half", [P, T])
        zeros = sb("zeros", [P, T])
        ones = sb("ones", [P, 1])
        lo_sum = sb("lo_sum", [P, 4])
        lo_any = sb("lo_any", [P, 4])
        lo_flag = sb("lo_flag", [1, 1])
        warm = sb("warm", [P, 1])

        N0 = sb("N0", [P, T, D])
        NF = sb("NF", [P, T, D])
        n_tok = [sb(f"n_tok_{h}", [P, T, D], f32r) for h in ("hi", "lo")]
        N0B1 = sb("N0B1", [P, T, D])
        N0B2 = sb("N0B2", [P, T, D])
        X1 = sb("X1", [P, T, D])
        YF = sb("YF", [P, T, D])
        aT = [sb(f"aT_{h}", [P, N], f32r) for h in ("hi", "lo")]
        yT = [sb(f"yT_{h}", [P, N], f32r) for h in ("hi", "lo")]
        WT = {L: [sb(f"{L}T_{h}", [P, N], f32r) for h in ("hi", "lo")] for L in ("h1", "h2")}
        SC = [sb(f"sc_{h}", [P, SEQS, 3, P], f32r) for h in ("hi", "lo")]
        SLOTS = 6
        HA = [sb(f"attn_hidden_{h}", [P, SLOTS, N], f32r) for h in ("hi", "lo")]
        SLOT0 = {"h1": 0, "h2": J, "fm": 2 * J}
        HG = [sb(f"ffn_gate_{h}", [P, J, N], f32r) for h in ("hi", "lo")]
        HF = [sb(f"ffn_h1_{h}", [P, J, N], f32r) for h in ("hi", "lo")]
        TH = sb("TH", [P, N])
        FN = raw_a[:, 0:N].rearrange("p (t d) -> p t d", t=T)
        OTA = sb("OTA", [P, N])
        OTF = sb("OTF", [P, N])

        def ln_tiles(name):
            return {"st": sb(f"{name}_st", [P, T, 6]), "mv": sb(f"{name}_mv", [P, T, 2]),
                    "ve": sb(f"{name}_ve", [P, T]), "r": sb(f"{name}_r", [P, T]), "nmr": sb(f"{name}_nmr", [P, T])}

        LN = {k: ln_tiles(f"ln_{k}") for k in ("x", "t", "x1", "o", "y", "f")}
        hv = sb("ln_xx_var", [P, T])
        hd = sb("ln_xx_ve", [P, T])
        hr = sb("ln_xx_r", [P, T])

        bank_of = [ctx.enter_context(nc.psum_tensor(f"bank{i}", [P, N], f32)) for i in range(8)]
        BANKS = {"nT": 2, "h1u0": 4, "fT": 6, "h1u1": 0, "h2u0": 7, "h1d": 1, "h1u2": 3, "h1u3": 5, "h2u1": 7, "h2d": 2,
                 "h2u2": 3, "yT": 5, "h2u3": 4, "p0": 7, "q0": 0, "p1": 3, "p2": 5, "q1": 4, "q2": 1, "s0": 0, "s1": 2,
                 "p3": 0, "q3": 3, "t": 2, "h1_0": 5, "h1_1": 7, "h1_2": 3, "h1_3": 5, "h2_0": 4, "h2_1": 7, "mT": 1,
                 "h2_2": 5, "fmu0": 0, "fmu1": 3, "fmu2": 7, "h2_3": 1, "fmu3": 0, "fmd": 4, "oT": 0, "w3": 7}

        def bank(group):
            return bank_of[BANKS[group]]

        x_first, x_rest = sem("x_first"), sem("x_rest")
        PIECES = [("a", 0, 2 * DI), ("a", 2 * DI, 4 * DI), ("a", 4 * DI, 6 * DI),
                  ("f", F_W1, F_H1), ("f", F_H1, F_H2), ("f", F_H2, F_H2 + 2 * DI), ("f", F_H2 + 2 * DI, F_H2 + J * DI)]
        w_in = [sem(f"w_in{k}") for k in range(len(PIECES))]
        consts_ready = sem("consts_ready")
        dve_consts = sem("dve_consts")
        split_hi, split_lo_a, split_lo_f = sem("split_hi"), sem("split_lo_a"), sem("split_lo_f")
        lo_summed, lo_tested, lo_counted, lo_flagged = (sem(s) for s in ("lo_summed", "lo_tested", "lo_counted", "lo_flagged"))
        stored = sem("stored")

        lo_names = lambda L: " ".join(f"{L}_lo{j}" for j in range(J))
        head_vector = Milestones(sem("head_vector"), "stats aggr n0 nf")
        head_pool = Milestones(sem("head_pool"), "ve r n0g vr v0 ve0 r0 n0b1 n_lo")
        head_scalar = Milestones(sem("head_scalar"), "n_hi")
        attn_tensor = Milestones(sem("attn_tensor"), "nT h1u0 h1u1 h2u0 h1u2 h1u3 h2u1 h2u2 h2u3 h1d h2d s0 s1 t mT fmu0 fmu1 fmu2 fmu3 fmd oT")
        attn_scalar = Milestones(sem("attn_scalar"),
            "nT_hi h1_hi0 h1_g0 h1_hi1 h1_g1 h2_hi0 h2_g0 h1_hi2 h1_g2 h1_hi3 h1_g3 h2_hi1 h2_g1 h2_hi2 h2_g2 "
            "h2_hi3 h2_g3 h1T_hi h2T_hi s_hi0 s_hi1 t mT_hi mT_g fm_hi0 fm_g0 fm_hi1 fm_g1 fm_hi2 fm_g2 fm_hi3 "
            "fm_g3 fm_out")
        attn_vector = Milestones(sem("attn_vector"),
            "nT_lo h1_lo0 h2_lo0 h1_lo1 h1_lo2 h1_lo3 h2_lo1 h2_lo2 h2_lo3 h1T_lo h2T_lo s_mask0 s_mask1 s_lo0 "
            "s_lo1 t_stats t_aggr t_g x1 x1_stats x1_aggr m mT_lo fm_lo0 fm_lo1 fm_lo2 fm_lo3 out o_stats o_aggr")
        attn_pool = Milestones(sem("attn_pool"), "n0b2 t_ve t_r x1_ve x1_r o_ve o_r")
        ffn_tensor = Milestones(sem("ffn_tensor"), "yT p0 q0 p1 p2 q1 q2 p3 q3 h1_0 h1_1 h1_2 h1_3 h2_0 h2_1 h2_2 h2_3 w3")
        ffn_scalar = Milestones(sem("ffn_scalar"),
            "yT_hi th0 g_hi0 th1 th2 g_hi1 th3 g_hi2 g_hi3 h1_hi0 h1_g0 h1_hi1 h1_g1 h1_hi2 h1_g2 h1_hi3 h1_g3 "
            "h2_hi0 h2_g0 h2_hi1 h2_g1 h2_hi2 h2_g2 h2_hi3 h2_g3 w3")
        ffn_vector = Milestones(sem("ffn_vector"),
            "on y_stats y_aggr y yT_lo u0 g0 g_lo0 u1 g1 u2 g2 g_lo1 u3 g3 g_lo2 g_lo3 h1_lo0 h1_lo1 h1_lo2 "
            "h1_lo3 h2_lo0 h2_lo1 h2_lo2 h2_lo3")
        ffn_pool = Milestones(sem("ffn_pool"), "xo y_ve y_r")
        end_tensor = Milestones(sem("end_tensor"), "fT")
        end_vector = Milestones(sem("end_vector"), "f_stats f_aggr")
        end_pool = Milestones(sem("end_pool"), "f_ve f_r f_mr f_nmr xf", base=1)
        end_scalar = Milestones(sem("end_scalar"), "fn", base=1)
        READ_BY = {"nT": (attn_vector, "nT_lo"), "mT": (attn_vector, "mT_lo"), "oT": (attn_vector, "out"),
                   "h1d": (attn_vector, "h1T_lo"), "h2d": (attn_vector, "h2T_lo"), "fmd": (attn_scalar, "fm_out"),
                   "s0": (attn_vector, "s_lo0"), "s1": (attn_vector, "s_lo1"), "t": (attn_vector, "t_g"),
                   "yT": (ffn_vector, "yT_lo"), "w3": (ffn_scalar, "w3"), "fT": (end_scalar, "fn")}
        for j in range(J):
            READ_BY |= {f"{L}u{j}": (attn_vector, f"{L}_lo{j}") for L in ("h1", "h2", "fm")}
            READ_BY |= {f"p{j}": (ffn_vector, f"u{j}"), f"q{j}": (ffn_vector, f"g_lo{j}"),
                        f"h1_{j}": (ffn_vector, f"h1_lo{j}"), f"h2_{j}": (ffn_vector, f"h2_lo{j}")}
        params_in = sem("params_in")
        dve_waited, pool_waited = sem("dve_waited"), sem("pool_waited")

        def piece_dst(k, half):
            kind, c0, c1 = PIECES[k]
            return (Aw if kind == "a" else Fw)[half][:, c0:c1]

        def piece_raw(k):
            kind, c0, c1 = PIECES[k]
            if kind == "a":
                return raw_a[:, c0:c1]
            return [raw_b[:, 0:3 * DI], raw_a[:, 0:4 * DI], raw_a[:, 4 * DI:6 * DI], raw_b[:, 0:2 * DI]][k - 3]

        def flat(ap):
            return ap.rearrange("p t d -> p (t d)")

        def on(chunk, step, *args):
            if chunk is not None:
                step(*args, chunk)

        def row(r):
            return bc[:, r:r + 1, :].broadcast_to([P, T, D])

        block = ctx.enter_context(nc.Block())

        @block.sync
        def _(sp):
            xv = x.rearrange("b (s p) d -> p (b s) d", p=P)
            ov = out.rearrange("b (s p) d -> p (b s) d", p=P)
            sp.dma_start(X[:, 0:T, :], xv[:, 0:T, :]).then_inc(x_first, 16)
            sp.dma_start(piece_raw(0), attn_w[:, 0:2 * DI]).then_inc(w_in[0], 16)
            sp.dma_start(piece_raw(1), attn_w[:, 2 * DI:4 * DI]).then_inc(w_in[1], 16)
            sp.dma_start(piece_raw(2), attn_w[:, 4 * DI:6 * DI]).then_inc(w_in[2], 16)
            sp.dma_start(piece_raw(3), ffn_w[:, F_W1:F_H1]).then_inc(w_in[3], 16)
            sp.dma_start(X[:, T:TILES, :], xv[:, T:TILES, :]).then_inc(x_rest, 16)
            for k in range(4, len(PIECES)):
                sp.wait_ge(split_hi, 4 if k == 6 else 3)
                if k == 6:
                    sp.wait_ge(split_lo_f, 1)
                else:
                    sp.wait_ge(split_lo_a, 3)
                _, c0, c1 = PIECES[k]
                sp.dma_start(piece_raw(k), ffn_w[:, c0:c1]).then_inc(w_in[k], 16)
            for c in range(CHUNKS):
                sp.wait_ge(end_pool.sem, end_pool.after("xf", c))
                sp.dma_start(ov[:, c * T:(c + 1) * T, :], X[:, c * T:(c + 1) * T, :]).then_inc(stored, 16)
            sp.wait_ge(stored, 16 * CHUNKS)

        @block.gpsimd
        def _(pool):
            pool.dma_start(cols[:, :], columns).then_inc(params_in, 16)
            pool.dma_start(bc[:, :, :], rows.rearrange("(o r) d -> o r d", o=1).broadcast_to([P, 3, D])).then_inc(params_in, 16)
            nc.gpsimd.memset(eps[:, :], EPS)
            nc.gpsimd.memset(neg_half[:, :], -0.5)
            nc.gpsimd.memset(zeros[:, :], 0.0)
            nc.gpsimd.memset(ones[:, :], 1.0)
            nc.gpsimd.memset(ident[:, :], 0.0)
            nc.gpsimd.memset(mask[:, :, :], 1.0).then_inc(consts_ready, 1)
            pool.sem_inc(end_pool.sem, end_pool.base)
            pool.wait_ge(consts_ready, 1)
            nc.gpsimd.affine_select(out=ident[:, :], in_=ident[:, :], compare_op=ALU.not_equal, fill=1.0,
                                    base=0, pattern=[[-1, P]], channel_multiplier=1).then_inc(consts_ready, 1)
            for k in (0, 1):
                nc.gpsimd.affine_select(out=mask[:, k, :], in_=mask[:, k, :], compare_op=ALU.is_ge, fill=0.0,
                                        base=0, pattern=[[1, P]], channel_multiplier=-1).then_inc(consts_ready, 1)
            pool.wait_ge(params_in, 32)

            def rstd(ms, name, ln, aggr_sem, aggr_value, chunk):
                pool.wait_ge(aggr_sem, aggr_value)
                nc.gpsimd.tensor_tensor(ln["ve"][:, :], ln["mv"][:, :, 1], eps[:, :], ALU.add).then_inc(ms.sem, ms.step(f"{name}ve"))
                pool.wait_ge(ms.sem, ms.after(f"{name}ve", chunk))
                nc.gpsimd.tensor_tensor(ln["r"][:, :], ln["ve"][:, :], neg_half[:, :], ALU.pow).then_inc(ms.sem, ms.step(f"{name}r"))

            def head_rstd(c):
                rstd(head_pool, "", LN["x"], head_vector.sem, head_vector.after("aggr", c), c)

            def head_rstd2(c):
                ms = head_pool
                pool.wait_ge(ms.sem, ms.after("r", c))
                nc.gpsimd.tensor_tensor(hv[:, :], LN["x"]["mv"][:, :, 1], LN["x"]["r"][:, :], ALU.mult).then_inc(ms.sem, ms.step("vr"))
                pool.wait_ge(ms.sem, ms.after("vr", c))
                nc.gpsimd.tensor_tensor(hd[:, :], hv[:, :], LN["x"]["r"][:, :], ALU.mult).then_inc(ms.sem, ms.step("v0"))
                pool.wait_ge(ms.sem, ms.after("v0", c))
                nc.gpsimd.tensor_tensor(hv[:, :], hd[:, :], eps[:, :], ALU.add).then_inc(ms.sem, ms.step("ve0"))
                pool.wait_ge(ms.sem, ms.after("ve0", c))
                nc.gpsimd.tensor_tensor(hr[:, :], hv[:, :], neg_half[:, :], ALU.pow).then_inc(ms.sem, ms.step("r0"))

            def head_scaled(c):
                ms = head_pool
                pool.wait_ge(head_vector.sem, head_vector.after("n0", c))
                nc.gpsimd.tensor_tensor(NF[:, :, :], N0[:, :, :], row(R_G), ALU.mult).then_inc(ms.sem, ms.step("n0g"))

            def head_shifted(c):
                ms = head_pool
                pool.wait_ge(head_vector.sem, head_vector.after("n0", c))
                if not (isinstance(c, int) and c == 0):
                    pool.wait_ge(attn_vector.sem, attn_vector.after("x1", c - 1))
                nc.gpsimd.tensor_tensor(N0B1[:, :, :], N0[:, :, :], row(R_B), ALU.add).then_inc(ms.sem, ms.step("n0b1"))

            def head_low(c):
                ms = head_pool
                pool.wait_ge(head_scalar.sem, head_scalar.after("n_hi", c))
                nc.gpsimd.tensor_tensor(n_tok[1][:, :, :], NF[:, :, :], n_tok[0][:, :, :].bitcast(f32), ALU.subtract)\
                    .then_inc(ms.sem, ms.step("n_lo"))

            def x_after_attention(f):
                pool.wait_ge(ffn_vector.sem, ffn_vector.after("on", f))
                nc.gpsimd.sem_inc(pool_waited, 1)
                xc = X[:, bass.ds(f * T, T), :]
                nc.gpsimd.tensor_tensor(xc, xc, X1[:, :, :], ALU.add).then_inc(ffn_pool.sem, ffn_pool.step("xo"))

            def split(k):
                pool.wait_ge(split_hi, k + 1)
                nc.gpsimd.tensor_tensor(piece_dst(k, 1), piece_raw(k), piece_dst(k, 0).bitcast(f32), ALU.subtract)\
                    .then_inc(split_lo_f, 1)

            def residual_b2(a):
                pool.wait_ge(head_vector.sem, head_vector.after("n0", a))
                if not (isinstance(a, int) and a == 0):
                    pool.wait_ge(attn_vector.sem, attn_vector.after("out", a - 1))
                nc.gpsimd.tensor_tensor(N0B2[:, :, :], N0[:, :, :], row(R_B2), ALU.add).then_inc(attn_pool.sem, attn_pool.step("n0b2"))

            def attn_rstd(name, a):
                rstd(attn_pool, f"{name}_", LN[name], attn_vector.sem, attn_vector.after(f"{name}_aggr", a), a)

            def y_rstd(f):
                rstd(ffn_pool, "y_", LN["y"], ffn_vector.sem, ffn_vector.after("y_aggr", f), f)

            def end_rstd(e):
                ms, ln = end_pool, LN["f"]
                rstd(ms, "f_", ln, end_vector.sem, end_vector.after("f_aggr", e), e)
                pool.wait_ge(ms.sem, ms.after("f_r", e))
                nc.gpsimd.tensor_tensor(ln["ve"][:, :], ln["mv"][:, :, 0], ln["r"][:, :], ALU.mult).then_inc(ms.sem, ms.step("f_mr"))
                pool.wait_ge(ms.sem, ms.after("f_mr", e))
                nc.gpsimd.tensor_tensor(ln["nmr"][:, :], zeros[:, :], ln["ve"][:, :], ALU.subtract).then_inc(ms.sem, ms.step("f_nmr"))

            def end_sum(e):
                pool.wait_ge(end_scalar.sem, end_scalar.after("fn", e))
                nc.gpsimd.sem_inc(pool_waited, 1)
                xc = X[:, bass.ds(e * T, T), :]
                nc.gpsimd.tensor_tensor(xc, xc, FN[:, :, :], ALU.add).then_inc(end_pool.sem, end_pool.step("xf"))

            def iteration(e, f, a, h):
                on(f, x_after_attention)
                on(f, y_rstd)
                if f is None and a is not None:
                    for k in range(3, len(PIECES)):
                        split(k)
                on(e, end_rstd)
                on(h, head_rstd)
                on(a, residual_b2)
                on(a, attn_rstd, "t")
                on(a, attn_rstd, "x1")
                on(h, head_scaled)
                on(h, head_rstd2)
                on(e, end_sum)
                on(h, head_shifted)
                on(a, attn_rstd, "o")
                on(h, head_low)

            for step in (head_rstd, head_scaled, head_rstd2, head_shifted, head_low):
                step(0)
            iteration(None, None, 0, 1)
            iteration(None, 0, 1, 2)
            with pool.Fori(1, CHUNKS - 2) as i:
                iteration(i - 1, i, i + 1, i + 2)
            iteration(CHUNKS - 3, CHUNKS - 2, CHUNKS - 1, None)
            iteration(CHUNKS - 2, CHUNKS - 1, None, None)
            iteration(CHUNKS - 1, None, None, None)
        @block.scalar
        def _(act):
            act.wait_ge(consts_ready, 1)
            nc.scalar.activation(warm[:, :], ones[:, :], ACT.Gelu).then_inc(end_scalar.sem, end_scalar.base)
            for k in range(3):
                act.wait_ge(w_in[k], 16)
                nc.scalar.activation(piece_dst(k, 0), piece_raw(k), ACT.Copy).then_inc(split_hi, 1)
            act.wait_ge(params_in, 32)

            def head(c):
                if not (isinstance(c, int) and c == 0):
                    act.wait_ge(attn_tensor.sem, attn_tensor.after("t", c - 1))
                act.wait_ge(head_vector.sem, head_vector.after("nf", c))
                nc.scalar.activation(n_tok[0][:, :, :], NF[:, :, :], ACT.Copy).then_inc(head_scalar.sem, head_scalar.step("n_hi"))

            def hi_copy(ms, name, tensor, group, dst, chunk):
                act.wait_ge(tensor.sem, tensor.after(group, chunk))
                nc.scalar.activation(dst, bank(group)[:, :], ACT.Copy).then_inc(ms.sem, ms.step(name))

            def gelu(ms, L, j, tensor, group, dst, chunk, **affine):
                act.wait_ge(tensor.sem, tensor.after(group, chunk))
                nc.scalar.activation(dst, bank(group)[:, :], ACT.Gelu, **affine).then_inc(ms.sem, ms.step(f"{L}_hi{j}"))
                act.wait_ge(ms.sem, ms.after(f"{L}_hi{j}", chunk))
                nc.scalar.activation(bank(group)[:, :], bank(group)[:, :], ACT.Gelu, **affine).then_inc(ms.sem, ms.step(f"{L}_g{j}"))

            def up(L, j, a):
                slot = (SLOT0[L] + j) % SLOTS
                gelu(attn_scalar, L, j, attn_tensor, f"{L}u{j}", HA[0][:, slot, :], a,
                     bias=cols[:, C_B1[L] + j:C_B1[L] + j + 1])

            def down(L, a):
                act.wait_ge(attn_tensor.sem, attn_tensor.after(f"{L}d", a))
                nc.scalar.activation(WT[L][0][:, :], bank(f"{L}d")[:, :], ACT.Identity,
                                     bias=cols[:, C_B2[L]:C_B2[L] + 1]).then_inc(attn_scalar.sem, attn_scalar.step(f"{L}T_hi"))

            def scores(b, a):
                act.wait_ge(attn_vector.sem, attn_vector.after(f"s_mask{b}", a))
                nc.scalar.activation(flat(SC[0][:, b, :, :]), bank(f"s{b}")[:, 0:3 * P], ACT.Copy)\
                    .then_inc(attn_scalar.sem, attn_scalar.step(f"s_hi{b}"))

            def t_gelu(a):
                act.wait_ge(attn_tensor.sem, attn_tensor.after("t", a))
                nc.scalar.activation(bank("t")[:, :], bank("t")[:, :], ACT.Gelu).then_inc(attn_scalar.sem, attn_scalar.step("t"))

            def m_transposed(a):
                act.wait_ge(attn_tensor.sem, attn_tensor.after("mT", a))
                g, b = cols[:, C_G:C_G + 1], cols[:, C_B:C_B + 1]
                nc.scalar.activation(aT[0][:, :], bank("mT")[:, :], ACT.Identity, scale=g, bias=b)\
                    .then_inc(attn_scalar.sem, attn_scalar.step("mT_hi"))
                act.wait_ge(attn_scalar.sem, attn_scalar.after("mT_hi", a))
                nc.scalar.activation(bank("mT")[:, :], bank("mT")[:, :], ACT.Identity, scale=g, bias=b)\
                    .then_inc(attn_scalar.sem, attn_scalar.step("mT_g"))

            def tanh(j, f):
                if j:
                    act.wait_ge(ffn_vector.sem, ffn_vector.after(f"g{j - 1}", f))
                act.wait_ge(ffn_tensor.sem, ffn_tensor.after(f"p{j}", f))
                nc.scalar.activation(TH[:, :], bank(f"p{j}")[:, :], ACT.Tanh, scale=gate_half[:, j:j + 1])\
                    .then_inc(ffn_scalar.sem, ffn_scalar.step(f"th{j}"))

            def gate_hi(j, f):
                act.wait_ge(ffn_vector.sem, ffn_vector.after(f"g{j}", f))
                nc.scalar.activation(HG[0][:, j, :], bank(f"q{j}")[:, :], ACT.Copy)\
                    .then_inc(ffn_scalar.sem, ffn_scalar.step(f"g_hi{j}"))

            def layer(L, j, f):
                dst = HF if L == "h1" else HG
                gelu(ffn_scalar, L, j, ffn_tensor, f"{L}_{j}", dst[0][:, j, :], f,
                     scale=cols[:, C_HS[L] + j:C_HS[L] + j + 1])

            def n_transposed(a):
                hi_copy(attn_scalar, "nT_hi", attn_tensor, "nT", aT[0][:, :], a)

            def y_transposed(f):
                hi_copy(ffn_scalar, "yT_hi", ffn_tensor, "yT", yT[0][:, :], f)

            def fm_out(a):
                act.wait_ge(attn_tensor.sem, attn_tensor.after("fmd", a))
                nc.scalar.activation(OTA[:, :], bank("fmd")[:, :], ACT.Copy).then_inc(attn_scalar.sem, attn_scalar.step("fm_out"))

            def w3_out(f):
                if not (isinstance(f, int) and f == 0):
                    act.wait_ge(end_tensor.sem, end_tensor.after("fT", f - 1))
                act.wait_ge(ffn_tensor.sem, ffn_tensor.after("w3", f))
                nc.scalar.activation(OTF[:, :], bank("w3")[:, :], ACT.Copy, scale=cols[:, C_S3:C_S3 + 1])\
                    .then_inc(ffn_scalar.sem, ffn_scalar.step("w3"))

            def end_normalise(e):
                if not (isinstance(e, int) and e == 0):
                    act.wait_ge(end_pool.sem, end_pool.after("xf", e - 1))
                act.wait_ge(end_pool.sem, end_pool.after("f_nmr", e))
                for t in range(T):
                    last = nc.scalar.activation(FN[:, t, :], bank("fT")[:, t * P:(t + 1) * P], ACT.Identity,
                                                scale=LN["f"]["r"][:, t:t + 1], bias=LN["f"]["nmr"][:, t:t + 1])
                last.then_inc(end_scalar.sem, end_scalar.step("fn"))

            def split_ffn_weights():
                for k in range(3, len(PIECES)):
                    act.wait_ge(w_in[k], 16)
                    nc.scalar.activation(piece_dst(k, 0), piece_raw(k), ACT.Copy).then_inc(split_hi, 1)

            def sum_low_parts():
                for k in range(3, len(PIECES)):
                    act.wait_ge(split_lo_f, len(PIECES) - 3)
                    if k == len(PIECES) - 1:
                        act.wait_ge(lo_summed, k - 3)
                    nc.scalar.activation(piece_raw(k), piece_dst(k, 1).bitcast(f32), ACT.Abs,
                                         accum_out=lo_sum[:, k - 3:k - 2]).then_inc(lo_summed, 1)

            def iteration(e, f, a, h):
                on(a, n_transposed)
                on(a, up, "h1", 0)
                on(a, up, "h1", 1)
                on(a, up, "h2", 0)
                on(a, up, "h1", 2)
                on(a, up, "h1", 3)
                on(a, up, "h2", 1)
                on(a, up, "h2", 2)
                on(f, y_transposed)
                on(a, up, "h2", 3)
                if f is None and a is not None:
                    split_ffn_weights()
                on(f, tanh, 0)
                on(a, down, "h1")
                on(f, gate_hi, 0)
                on(a, down, "h2")
                on(f, tanh, 1)
                on(e, end_normalise)
                on(a, scores, 0)
                on(f, tanh, 2)
                on(f, gate_hi, 1)
                on(a, scores, 1)
                on(f, tanh, 3)
                on(f, gate_hi, 2)
                on(f, gate_hi, 3)
                on(a, t_gelu)
                if f is None and a is not None:
                    sum_low_parts()
                on(f, layer, "h1", 0)
                on(f, layer, "h1", 1)
                on(f, layer, "h1", 2)
                on(f, layer, "h1", 3)
                on(f, layer, "h2", 0)
                on(a, m_transposed)
                on(f, layer, "h2", 1)
                on(a, up, "fm", 0)
                on(a, up, "fm", 1)
                on(a, up, "fm", 2)
                on(a, up, "fm", 3)
                on(f, layer, "h2", 2)
                on(a, fm_out)
                on(f, layer, "h2", 3)
                on(h, head)
                on(f, w3_out)

            head(0)
            iteration(None, None, 0, 1)
            iteration(None, 0, 1, 2)
            with act.Fori(1, CHUNKS - 2) as i:
                iteration(i - 1, i, i + 1, i + 2)
            iteration(CHUNKS - 3, CHUNKS - 2, CHUNKS - 1, None)
            iteration(CHUNKS - 2, CHUNKS - 1, None, None)
            iteration(CHUNKS - 1, None, None, None)
        @block.vector
        def _(dve):
            def alone():
                nc.vector.sem_inc(dve_waited, 1)

            def stats(ms, name, src, ln, chunk):
                for t in range(T):
                    last = nc.vector.bn_stats(ln["st"][:, t, :], src(t))
                last.then_inc(ms.sem, ms.step(f"{name}stats"))
                dve.wait_ge(ms.sem, ms.after(f"{name}stats", chunk))
                alone()
                for t in range(T):
                    last = nc.vector.bn_aggr(ln["mv"][:, t, :], ln["st"][:, t, :])
                last.then_inc(ms.sem, ms.step(f"{name}aggr"))

            def normalise(ms, name, dst, src, ln):
                for t in range(T):
                    last = nc.vector.tensor_scalar(dst(t), src(t), ln["mv"][:, t, 0:1], ln["r"][:, t:t + 1],
                                                   ALU.subtract, ALU.mult)
                last.then_inc(ms.sem, ms.step(name))

            def x_tile(c):
                return lambda t: X[:, c * T + t, :]

            def tile_of(buf):
                return lambda t: buf[:, t, :]

            def low(ms, name, dst, whole, high):
                nc.vector.tensor_tensor(dst, whole, high.bitcast(f32), ALU.subtract).then_inc(ms.sem, ms.step(name))

            def head_stats(c):
                if not (isinstance(c, int) and c == 0):
                    dve.wait_ge(head_pool.sem, head_pool.after("n0b1", c - 1))
                    alone()
                stats(head_vector, "", x_tile(c), LN["x"], c)

            def head_n0(c):
                ms = head_vector
                first = isinstance(c, int) and c == 0
                if not first:
                    dve.wait_ge(attn_pool.sem, attn_pool.after("n0b2", c - 1))
                dve.wait_ge(head_pool.sem, head_pool.after("r", c))
                normalise(ms, "n0", tile_of(N0), x_tile(c), LN["x"])

            def head_n(c):
                ms = head_vector
                dve.wait_ge(head_pool.sem, head_pool.after("n0g", c))
                dve.wait_ge(head_pool.sem, head_pool.after("r0", c))
                for t in range(T):
                    last = nc.vector.scalar_tensor_tensor(NF[:, t, :], NF[:, t, :], hr[:, t:t + 1], bc[:, R_B, :],
                                                          ALU.mult, ALU.add)
                last.then_inc(ms.sem, ms.step("nf"))

            def attn_low(name, scalar_step, dst, group, high, a):
                dve.wait_ge(attn_scalar.sem, attn_scalar.after(scalar_step, a))
                low(attn_vector, name, dst, bank(group)[:, :], high)

            def up_low(L, j, a):
                slot = (SLOT0[L] + j) % SLOTS
                attn_low(f"{L}_lo{j}", f"{L}_g{j}", HA[1][:, slot, :], f"{L}u{j}", HA[0][:, slot, :], a)

            def down_low(L, a):
                dve.wait_ge(attn_scalar.sem, attn_scalar.after(f"{L}T_hi", a))
                nc.vector.scalar_tensor_tensor(WT[L][1][:, :], bank(f"{L}d")[:, :], cols[:, C_B2[L]:C_B2[L] + 1],
                                               WT[L][0][:, :].bitcast(f32), ALU.add, ALU.subtract)\
                    .then_inc(attn_vector.sem, attn_vector.step(f"{L}T_lo"))

            def score_mask(b, a):
                dve.wait_ge(attn_tensor.sem, attn_tensor.after(f"s{b}", a))
                diagonal = bank(f"s{b}")[:, 0:4 * P].rearrange("p (k z) -> p k z", k=4)[:, 0:3:2, :]
                nc.vector.tensor_tensor(diagonal, diagonal, mask[:, :, :], ALU.mult)\
                    .then_inc(attn_vector.sem, attn_vector.step(f"s_mask{b}"))

            def score_low(b, a):
                dve.wait_ge(attn_scalar.sem, attn_scalar.after(f"s_hi{b}", a))
                low(attn_vector, f"s_lo{b}", flat(SC[1][:, b, :, :]), bank(f"s{b}")[:, 0:3 * P], flat(SC[0][:, b, :, :]))

            tb = bank("t")[:, :].rearrange("p (t d) -> p t d", t=T)

            def t_stats(a):
                ms = attn_vector
                dve.wait_ge(attn_scalar.sem, attn_scalar.after("t", a))
                alone()
                stats(ms, "t_", tile_of(tb), LN["t"], a)

            def t_scaled(a):
                ms = attn_vector
                if not (isinstance(a, int) and a == 0):
                    dve.wait_ge(ffn_pool.sem, ffn_pool.after("xo", a - 1))
                dve.wait_ge(ms.sem, ms.after("t_aggr", a))
                for t in range(T):
                    last = nc.vector.scalar_tensor_tensor(X1[:, t, :], tb[:, t, :], LN["t"]["mv"][:, t, 0:1],
                                                          bc[:, R_G, :], ALU.subtract, ALU.mult)
                last.then_inc(ms.sem, ms.step("t_g"))

            def x1_sum(a):
                ms = attn_vector
                dve.wait_ge(head_pool.sem, head_pool.after("n0b1", a))
                dve.wait_ge(attn_pool.sem, attn_pool.after("t_r", a))
                dve.wait_ge(ms.sem, ms.after("t_g", a))
                for t in range(T):
                    last = nc.vector.scalar_tensor_tensor(X1[:, t, :], X1[:, t, :], LN["t"]["r"][:, t:t + 1],
                                                          N0B1[:, t, :], ALU.mult, ALU.add)
                last.then_inc(ms.sem, ms.step("x1"))

            def x1_stats(a):
                ms = attn_vector
                dve.wait_ge(ms.sem, ms.after("x1", a))
                alone()
                stats(ms, "x1_", tile_of(X1), LN["x1"], a)

            def m_norm(a):
                dve.wait_ge(attn_pool.sem, attn_pool.after("x1_r", a))
                normalise(attn_vector, "m", tile_of(X1), tile_of(X1), LN["x1"])

            def branch_out(a):
                ms = attn_vector
                dve.wait_ge(attn_pool.sem, attn_pool.after("n0b2", a))
                dve.wait_ge(attn_tensor.sem, attn_tensor.after("oT", a))
                nc.vector.tensor_tensor(flat(X1[:, :, :]), bank("oT")[:, :], flat(N0B2[:, :, :]), ALU.add)\
                    .then_inc(ms.sem, ms.step("out"))

            def branch_stats(a):
                ms = attn_vector
                dve.wait_ge(ms.sem, ms.after("out", a))
                alone()
                stats(ms, "o_", tile_of(X1), LN["o"], a)

            def branch_norm(f):
                ms = ffn_vector
                dve.wait_ge(attn_pool.sem, attn_pool.after("o_r", f))
                normalise(ms, "on", tile_of(X1), tile_of(X1), LN["o"])

            def y_stats(f):
                dve.wait_ge(ffn_pool.sem, ffn_pool.after("xo", f))
                alone()
                stats(ffn_vector, "y_", x_tile(f), LN["y"], f)

            def y_norm(f):
                dve.wait_ge(ffn_pool.sem, ffn_pool.after("y_r", f))
                normalise(ffn_vector, "y", tile_of(YF), x_tile(f), LN["y"])

            def gate(j, f):
                ms = ffn_vector
                dve.wait_ge(ffn_tensor.sem, ffn_tensor.after(f"q{j}", f))
                dve.wait_ge(ffn_scalar.sem, ffn_scalar.after(f"th{j}", f))
                nc.vector.scalar_tensor_tensor(TH[:, :], TH[:, :], 1.0, bank(f"p{j}")[:, :], ALU.add, ALU.mult)\
                    .then_inc(ms.sem, ms.step(f"u{j}"))
                dve.wait_ge(ms.sem, ms.after(f"u{j}", f))
                nc.vector.scalar_tensor_tensor(bank(f"q{j}")[:, :], TH[:, :], gate_coef[:, j:j + 1], bank(f"q{j}")[:, :],
                                               ALU.mult, ALU.mult).then_inc(ms.sem, ms.step(f"g{j}"))

            def gate_low(j, f):
                dve.wait_ge(ffn_scalar.sem, ffn_scalar.after(f"g_hi{j}", f))
                low(ffn_vector, f"g_lo{j}", HG[1][:, j, :], bank(f"q{j}")[:, :], HG[0][:, j, :])

            def layer_low(L, j, f):
                buf = HF if L == "h1" else HG
                dve.wait_ge(ffn_scalar.sem, ffn_scalar.after(f"{L}_g{j}", f))
                low(ffn_vector, f"{L}_lo{j}", buf[1][:, j, :], bank(f"{L}_{j}")[:, :], buf[0][:, j, :])

            def y_low(f):
                dve.wait_ge(ffn_scalar.sem, ffn_scalar.after("yT_hi", f))
                low(ffn_vector, "yT_lo", yT[1][:, :], bank("yT")[:, :], yT[0][:, :])

            def end_stats(e):
                if not (isinstance(e, int) and e == 0):
                    dve.wait_ge(end_scalar.sem, end_scalar.after("fn", e - 1))
                    alone()
                dve.wait_ge(end_tensor.sem, end_tensor.after("fT", e))
                alone()
                fT = bank("fT")[:, :].rearrange("p (t d) -> p t d", t=T)
                stats(end_vector, "f_", tile_of(fT), LN["f"], e)

            def iteration(e, f, a, h):
                on(a, attn_low, "nT_lo", "nT_hi", aT[1][:, :], "nT", aT[0][:, :])
                on(f, branch_norm)
                on(e, end_stats)
                on(a, up_low, "h1", 0)
                on(f, y_stats)
                on(a, up_low, "h2", 0)
                on(a, up_low, "h1", 1)
                on(a, up_low, "h1", 2)
                on(f, y_norm)
                on(a, up_low, "h1", 3)
                on(h, head_stats)
                on(a, up_low, "h2", 1)
                on(f, y_low)
                on(a, up_low, "h2", 2)
                on(a, up_low, "h2", 3)
                on(f, gate, 0)
                on(a, down_low, "h1")
                on(f, gate_low, 0)
                on(a, down_low, "h2")
                on(f, gate, 1)
                on(a, score_mask, 0)
                on(a, score_mask, 1)
                on(a, score_low, 0)
                on(f, gate, 2)
                on(a, score_low, 1)
                on(f, gate_low, 1)
                on(f, gate, 3)
                on(f, gate_low, 2)
                on(f, gate_low, 3)
                on(a, t_stats)
                on(a, t_scaled)
                on(f, layer_low, "h1", 0)
                on(a, x1_sum)
                on(f, layer_low, "h1", 1)
                on(a, x1_stats)
                on(f, layer_low, "h1", 2)
                on(f, layer_low, "h1", 3)
                on(a, m_norm)
                on(h, head_n0)
                on(f, layer_low, "h2", 0)
                on(a, attn_low, "mT_lo", "mT_g", aT[1][:, :], "mT", aT[0][:, :])
                on(f, layer_low, "h2", 1)
                on(h, head_n)
                on(a, up_low, "fm", 0)
                on(a, up_low, "fm", 1)
                on(a, up_low, "fm", 2)
                on(a, up_low, "fm", 3)
                on(f, layer_low, "h2", 2)
                on(a, branch_out)
                on(f, layer_low, "h2", 3)
                on(a, branch_stats)

            dve.wait_ge(params_in, 32)
            nc.vector.tensor_scalar(gate_half[:, :], cols[:, C_S1:C_S1 + J], 0.5, None, ALU.mult).then_inc(dve_consts, 1)
            dve.wait_ge(dve_consts, 1)
            nc.vector.tensor_tensor(gate_coef[:, :], gate_half[:, :], cols[:, C_S2:C_S2 + J], ALU.mult).then_inc(dve_consts, 1)
            dve.wait_ge(dve_consts, 2)
            dve.wait_ge(consts_ready, 4)
            dve.wait_ge(x_first, 16)
            alone()
            head_stats(0)
            head_n0(0)
            head_n(0)
            for k in range(3):
                dve.wait_ge(split_hi, k + 1)
                nc.vector.tensor_tensor(piece_dst(k, 1), piece_raw(k), piece_dst(k, 0).bitcast(f32), ALU.subtract)\
                    .then_inc(split_lo_a, 1)
            dve.wait_ge(x_rest, 16)
            iteration(None, None, 0, 1)
            dve.wait_ge(lo_summed, 4)
            nc.vector.tensor_scalar(lo_any[:, :], lo_sum[:, :], 0.0, None, ALU.not_equal).then_inc(lo_tested, 1)
            dve.wait_ge(lo_counted, 1)
            nc.vector.tensor_reduce(lo_flag[0:1, 0:1], bank_of[4][0:1, 0:4], mybir.AxisListType.X, ALU.add).then_inc(lo_flagged, 1)
            iteration(None, 0, 1, 2)
            with dve.Fori(1, CHUNKS - 2) as i:
                iteration(i - 1, i, i + 1, i + 2)
            iteration(CHUNKS - 3, CHUNKS - 2, CHUNKS - 1, None)
            iteration(CHUNKS - 2, CHUNKS - 1, None, None)
            iteration(CHUNKS - 1, None, None, None)
        @block.tensor
        def _(pe):
            LEAD = {"attn": 1, "ffn": 0, "end": -1}

            def stage(group):
                return "end" if group == "fT" else "ffn" if group[0] in "ypqw" or "_" in group else "attn"

            def bank_free(group, chunk):
                order = list(BANKS)
                n, back = order.index(group), 0
                while back <= 3:
                    n -= 1
                    if n < 0:
                        n, back = len(order) - 1, back + 1
                    if BANKS[order[n]] == BANKS[group]:
                        other = chunk + LEAD[stage(order[n])] - LEAD[stage(group)] - back
                        if not isinstance(other, int) or 0 <= other < CHUNKS:
                            ms, step = READ_BY[order[n]]
                            pe.wait_ge(ms.sem, ms.after(step, other))
                            return

            def transposes(ms, group, src, chunk):
                bank_free(group, chunk)
                for t in range(T):
                    last = nc.tensor.transpose(bank(group)[:, t * P:(t + 1) * P], src(t), ident[:, :])
                last.then_inc(ms.sem, ms.step(group))

            def n_transpose(a):
                pe.wait_ge(head_vector.sem, head_vector.after("nf", a))
                transposes(attn_tensor, "nT", lambda t: NF[:, t, :], a)

            def m_transpose(a):
                pe.wait_ge(attn_vector.sem, attn_vector.after("m", a))
                transposes(attn_tensor, "mT", lambda t: X1[:, t, :], a)

            def out_transpose(a):
                pe.wait_ge(attn_scalar.sem, attn_scalar.after("fm_out", a))
                transposes(attn_tensor, "oT", lambda t: OTA[:, t * P:(t + 1) * P], a)

            def y_transpose(f):
                pe.wait_ge(ffn_vector.sem, ffn_vector.after("y", f))
                transposes(ffn_tensor, "yT", lambda t: YF[:, t, :], f)

            def end_transpose(e):
                pe.wait_ge(ffn_scalar.sem, ffn_scalar.after("w3", e))
                transposes(end_tensor, "fT", lambda t: OTF[:, t * P:(t + 1) * P], e)

            def up(L, j, a):
                g = f"{L}u{j}"
                bank_free(g, a)
                if L != "h2" and j == 0 and isinstance(a, int) and a == 0:
                    pe.wait_ge(split_lo_a, 3 if L == "fm" else 1)
                if j == 0:
                    pe.wait_ge(attn_scalar.sem, attn_scalar.after("mT_hi" if L == "fm" else "nT_hi", a))
                w = slice(A_UP[L] + j * P, A_UP[L] + (j + 1) * P)
                nc.tensor.matmul(bank(g)[:, :], Aw[1][:, w], aT[0][:, :], start=True, stop=False)
                nc.tensor.matmul(bank(g)[:, :], Aw[0][:, w], aT[0][:, :], start=False, stop=False)
                if j == 0:
                    pe.wait_ge(attn_vector.sem, attn_vector.after("mT_lo" if L == "fm" else "nT_lo", a))
                nc.tensor.matmul(bank(g)[:, :], Aw[0][:, w], aT[1][:, :], start=False, stop=True)\
                    .then_inc(attn_tensor.sem, attn_tensor.step(g))

            def down(L, k, a):
                g = f"{L}d"
                if k == 0:
                    bank_free(g, a)
                    if L == "h1" and isinstance(a, int) and a == 0:
                        pe.wait_ge(split_lo_a, 2)
                w = slice(A_DOWN[L] + k * P, A_DOWN[L] + (k + 1) * P)
                slot = (SLOT0[L] + k) % SLOTS
                pe.wait_ge(attn_scalar.sem, attn_scalar.after(f"{L}_hi{k}", a))
                nc.tensor.matmul(bank(g)[:, :], Aw[1][:, w], HA[0][:, slot, :], start=(k == 0), stop=False)
                nc.tensor.matmul(bank(g)[:, :], Aw[0][:, w], HA[0][:, slot, :], start=False, stop=False)
                pe.wait_ge(attn_vector.sem, attn_vector.after(f"{L}_lo{k}", a))
                last = nc.tensor.matmul(bank(g)[:, :], Aw[0][:, w], HA[1][:, slot, :], start=False, stop=(k == J - 1))
                if k == J - 1:
                    last.then_inc(attn_tensor.sem, attn_tensor.step(g))

            def scores(b, a):
                g = f"s{b}"
                bank_free(g, a)
                if b == 0:
                    pe.wait_ge(attn_vector.sem, attn_vector.after("h2T_lo", a))
                o = b * S
                W1, W2 = WT["h1"], WT["h2"]
                for c0, s0, z0, z1 in ((0, o, o, o + S), (2 * P, o + P, o + P, o + S)):
                    for n, (x2, x1) in enumerate(((1, 0), (0, 0), (0, 1))):
                        last = nc.tensor.matmul(bank(g)[:, c0:c0 + z1 - z0], W2[x2][:, s0:s0 + P], W1[x1][:, z0:z1],
                                                start=(n == 0), stop=(n == 2))
                last.then_inc(attn_tensor.sem, attn_tensor.step(g))

            def t_product(a):
                bank_free("t", a)
                pe.wait_ge(head_pool.sem, head_pool.after("n_lo", a))
                for b in range(SEQS):
                    pe.wait_ge(attn_vector.sem, attn_vector.after(f"s_lo{b}", a))
                    for z, blocks in ((0, ((0, 0),)), (1, ((1, 0), (2, 1)))):
                        c0 = (2 * b + z) * P
                        steps = [(k, s, i, j) for k, s in blocks for i, j in ((1, 0), (0, 0), (0, 1))]
                        for n, (k, s, i, j) in enumerate(steps):
                            last = nc.tensor.matmul(bank("t")[:, c0:c0 + P], SC[i][:, b, k, :], n_tok[j][:, 2 * b + s, :],
                                                    start=(n == 0), stop=(n == len(steps) - 1))
                last.then_inc(attn_tensor.sem, attn_tensor.step("t"))

            def gate(x, j, lo_pass, f):
                g = f"{x}{j}"
                bank_free(g, f)
                base = {"p": F_W1, "q": F_W2}[x]
                w = slice(base + j * P, base + (j + 1) * P)
                if g == "p0":
                    pe.wait_ge(ffn_scalar.sem, ffn_scalar.after("yT_hi", f))
                if lo_pass:
                    nc.tensor.matmul(bank(g)[:, :], Fw[1][:, w], yT[0][:, :], start=True, stop=False)
                nc.tensor.matmul(bank(g)[:, :], Fw[0][:, w], yT[0][:, :], start=not lo_pass, stop=False)
                if g == "p0":
                    pe.wait_ge(ffn_vector.sem, ffn_vector.after("yT_lo", f))
                nc.tensor.matmul(bank(g)[:, :], Fw[0][:, w], yT[1][:, :], start=False, stop=True)\
                    .then_inc(ffn_tensor.sem, ffn_tensor.step(g))

            def layer(L, j, lo_pass, f):
                g = {"h1": f"h1_{j}", "h2": f"h2_{j}", "w3": "w3"}[L]
                src, base, width, of = {"h1": (HG, F_H1, DI, "g"), "h2": (HF, F_H2, DI, "h1"), "w3": (HG, F_W3, P, "h2")}[L]
                bank_free(g, f)
                order = [(half, k) for half in (0, 1) for k in range(J)] if j == 0 else \
                    [(half, k) for k in range(J) for half in (0, 1)]
                for n, (half, k) in enumerate(order):
                    if j == 0:
                        ms, name = ((ffn_vector, f"{of}_lo{k}") if half else (ffn_scalar, f"{of}_hi{k}"))
                        pe.wait_ge(ms.sem, ms.after(name, f))
                    w = slice(base + k * width + j * P, base + k * width + (j + 1) * P)
                    if lo_pass and not half:
                        nc.tensor.matmul(bank(g)[:, :], Fw[1][:, w], src[0][:, k, :], start=(n == 0), stop=False)
                    last = nc.tensor.matmul(bank(g)[:, :], Fw[0][:, w], src[half][:, k, :],
                                            start=(n == 0 and not lo_pass), stop=(n == 2 * J - 1))
                last.then_inc(ffn_tensor.sem, ffn_tensor.step(g))

            def iteration(e, f, a, lo_pass):
                on(a, n_transpose)
                on(a, up, "h1", 0)
                on(e, end_transpose)
                on(a, up, "h1", 1)
                on(a, up, "h2", 0)
                on(a, down, "h1", 0)
                on(a, up, "h1", 2)
                on(a, up, "h1", 3)
                on(a, up, "h2", 1)
                on(a, down, "h1", 1)
                on(a, down, "h2", 0)
                on(a, up, "h2", 2)
                on(f, y_transpose)
                on(a, down, "h1", 2)
                on(a, up, "h2", 3)
                on(a, down, "h2", 1)
                on(f, gate, "p", 0, lo_pass)
                on(f, gate, "q", 0, lo_pass)
                on(a, down, "h1", 3)
                on(f, gate, "p", 1, lo_pass)
                on(a, down, "h2", 2)
                on(a, down, "h2", 3)
                on(f, gate, "p", 2, lo_pass)
                on(f, gate, "q", 1, lo_pass)
                on(f, gate, "q", 2, lo_pass)
                on(a, scores, 0)
                on(a, scores, 1)
                on(f, gate, "p", 3, lo_pass)
                on(f, gate, "q", 3, lo_pass)
                on(a, t_product)
                on(f, layer, "h1", 0, lo_pass)
                on(f, layer, "h1", 1, lo_pass)
                on(f, layer, "h1", 2, lo_pass)
                on(f, layer, "h1", 3, lo_pass)
                on(f, layer, "h2", 0, lo_pass)
                on(f, layer, "h2", 1, lo_pass)
                on(a, m_transpose)
                on(f, layer, "h2", 2, lo_pass)
                on(a, up, "fm", 0)
                on(a, up, "fm", 1)
                on(a, up, "fm", 2)
                on(f, layer, "h2", 3, lo_pass)
                on(a, up, "fm", 3)
                on(a, down, "fm", 0)
                on(a, down, "fm", 1)
                on(a, down, "fm", 2)
                on(a, down, "fm", 3)
                on(a, out_transpose)
                on(f, layer, "w3", 0, lo_pass)

            pe.wait_ge(consts_ready, 4)
            iteration(None, None, 0, False)
            pe.wait_ge(split_lo_f, 4)
            pe.wait_ge(lo_tested, 1)
            nc.tensor.matmul(bank_of[4][0:1, 0:4], ones[:, :], lo_any[:, :], start=True, stop=True).then_inc(lo_counted, 1)
            pe.wait_ge(lo_flagged, 1)
            any_lo = pe.value_load(lo_flag[0:1, 0:1].bitcast(i32))

            def stream(lo_pass):
                iteration(None, 0, 1, lo_pass)
                with pe.Fori(1, CHUNKS - 2) as i:
                    iteration(i - 1, i, i + 1, lo_pass)
                iteration(CHUNKS - 3, CHUNKS - 2, CHUNKS - 1, lo_pass)
                iteration(CHUNKS - 2, CHUNKS - 1, None, lo_pass)
                iteration(CHUNKS - 1, None, None, lo_pass)

            with pe.If(any_lo > 0):
                stream(True)
            with pe.Else():
                stream(False)


def kernel(**inputs):
    import numpy as _np
    import concourse.bacc as _bacc
    from concourse import mybir as _mybir
    from concourse.bass_utils import run_bass_kernel_spmd as _run

    g = {k: _np.asarray(v) for k, v in inputs.items()}

    def k_tiles(w):
        return w.reshape(-1, 128, w.shape[1]).transpose(1, 0, 2).reshape(128, -1)

    def by_partition(v):
        return v.reshape(-1, 128).T

    a, f = "L0_attn_", "L0_ffn_"
    arrays = {
        "x": g[a + "x"],
        "attn_w": _np.concatenate([g[a + "h1_w1"], g[a + "h2_w1"], k_tiles(g[a + "h1_w2"]), k_tiles(g[a + "h2_w2"]),
                                   g[a + "fm_w1"], k_tiles(g[a + "fm_w2"])], axis=1),
        "ffn_w": _np.concatenate([k_tiles(g[f + n].T) for n in ("w1_w", "w2_w", "w3_w", "h1_w", "h2_w")], axis=1),
        "columns": _np.concatenate([by_partition(g[n]) for n in (
            a + "h1_b1", a + "h2_b1", a + "fm_b1", f + "w1_s", f + "w2_s", f + "h1_s", f + "h2_s",
            a + "h1_b2", a + "h2_b2", a + "ln_g", a + "ln_b", f + "w3_s")], axis=1),
        "rows": _np.stack([g[a + "ln_g"], g[a + "ln_b"], g[a + "fm_b2"]]),
    }
    nc = _bacc.Bacc("TRN2", target_bir_lowering=False, num_devices=1)
    args = []
    for name in arrays:
        arrays[name] = _np.ascontiguousarray(arrays[name])
        args.append(nc.dram_tensor(name, arrays[name].shape, _mybir.dt.from_np(arrays[name].dtype), kind="ExternalInput").ap())
    out = nc.dram_tensor("out", g[a + "x"].shape, _mybir.dt.from_np(g[a + "x"].dtype), kind="ExternalOutput").ap()
    sandwich_block(nc, *args, out)
    r = _run(nc, [arrays], core_ids=[0])
    return r.results[0]["out"]
```

```python
import concourse.bass as bass
from concourse import mybir
from contextlib import ExitStack


class Milestones:

    def __init__(self, **lines):
        self.lines = {key: [sem, names.split(), 0] for key, (sem, names) in lines.items()}

    def line(self, name):
        return next(line for line in self.lines.values() if name in line[1])

    def sem(self, name):
        return self.line(name)[0]

    def step(self, name):
        line = self.line(name)
        assert line[1][line[2] % len(line[1])] == name, (name, line)
        line[2] += 1
        return 1

    def after(self, name, chunk):
        _, names, _ = self.line(name)
        return chunk * len(names) + (len(names) + names.index(name) + 1)

    def start(self, engine):
        for sem, names, _ in self.lines.values():
            engine.sem_inc(sem, len(names))


def sandwich_block(nc, x, attn_w, ffn_w, columns, rows, out):
    f32, f32r, i32 = mybir.dt.float32, mybir.dt.float32r, mybir.dt.int32
    ALU, ACT = mybir.AluOpType, mybir.ActivationFunctionType

    P = 128
    B, S, D = x.shape
    TILES = B * S // P
    T = 4
    N = T * P
    CHUNKS = TILES // T
    SEQS = N // S
    DI = attn_w.shape[1] // 6
    J = DI // P
    EPS = 1e-5
    assert D == P and S == 2 * P and J == T

    A_UP = {"h1": 0, "h2": DI, "fm": 4 * DI}
    A_DOWN = {"h1": 2 * DI, "h2": 3 * DI, "fm": 5 * DI}
    F_W1, F_W2, F_W3, F_H1 = 0, DI, 2 * DI, 3 * DI
    F_H2 = F_H1 + J * DI
    C_B1 = {"h1": 0, "h2": J, "fm": 2 * J}
    C_S1, C_S2, C_HS = 3 * J, 4 * J, {"h1": 5 * J, "h2": 6 * J}
    C_B2 = {"h1": 7 * J, "h2": 7 * J + 1}
    C_G, C_B, C_S3 = 7 * J + 2, 7 * J + 3, 7 * J + 4
    R_G, R_B, R_B2 = range(3)

    ctx = ExitStack()
    with ctx:
        def sb(name, shape, dt=f32):
            return ctx.enter_context(nc.sbuf_tensor(name, shape, dt))

        def sem(name):
            return ctx.enter_context(nc.semaphore(name))

        X = sb("X", [P, TILES, D])
        Aw = [sb(f"attn_w_{h}", [P, 6 * DI], f32r) for h in ("hi", "lo")]
        Fw = [sb(f"ffn_w_{h}", [P, ffn_w.shape[1]], f32r) for h in ("hi", "lo")]
        raw_a = sb("raw_a", [P, 6 * DI])
        raw_b = sb("raw_b", [P, 3 * DI])
        cols = sb("cols", [P, columns.shape[1]])
        bc = sb("bc", [P, 3, D])
        gate_half = sb("gate_half", [P, J])
        gate_coef = sb("gate_coef", [P, J])
        ident = sb("ident", [P, P])
        mask = sb("mask", [P, 2, P])
        eps = sb("eps", [P, T])
        neg_half = sb("neg_half", [P, T])
        zeros = sb("zeros", [P, T])
        ones = sb("ones", [P, 1])
        lo_sum = sb("lo_sum", [P, 4])
        lo_any = sb("lo_any", [P, 4])
        lo_flag = sb("lo_flag", [1, 1])
        warm = sb("warm", [P, 1])

        N0 = sb("N0", [P, T, D])
        NF = sb("NF", [P, T, D])
        n_tok = [sb(f"n_tok_{h}", [P, T, D], f32r) for h in ("hi", "lo")]
        N0B1 = sb("N0B1", [P, T, D])
        N0B2 = sb("N0B2", [P, T, D])
        X1 = sb("X1", [P, T, D])
        aT = [sb(f"aT_{h}", [P, N], f32r) for h in ("hi", "lo")]
        mT = [sb(f"mT_{h}", [P, N], f32r) for h in ("hi", "lo")]
        yT = [sb(f"yT_{h}", [P, N], f32r) for h in ("hi", "lo")]
        WT = {L: [sb(f"{L}T_{h}", [P, N], f32r) for h in ("hi", "lo")] for L in ("h1", "h2")}
        SC = [sb(f"sc_{h}", [P, SEQS, 3, P], f32r) for h in ("hi", "lo")]
        SLOTS = 6
        HA = [sb(f"attn_hidden_{h}", [P, SLOTS, N], f32r) for h in ("hi", "lo")]
        SLOT0 = {"h1": 0, "h2": J, "fm": 2 * J}
        HG = [sb(f"ffn_gate_{h}", [P, J, N], f32r) for h in ("hi", "lo")]
        HF = [sb(f"ffn_h1_{h}", [P, J, N], f32r) for h in ("hi", "lo")]
        TH = sb("TH", [P, N])
        FN = raw_a[:, 0:N].rearrange("p (t d) -> p t d", t=T)
        YF = raw_a[:, N:2 * N].rearrange("p (t d) -> p t d", t=T)
        OTF = raw_a[:, 2 * N:3 * N]
        OTA = sb("OTA", [P, N])

        def ln_tiles(name):
            return {"st": sb(f"{name}_st", [P, T, 6]), "mv": sb(f"{name}_mv", [P, T, 2]),
                    "ve": sb(f"{name}_ve", [P, T]), "r": sb(f"{name}_r", [P, T]), "nmr": sb(f"{name}_nmr", [P, T])}

        LN = {k: ln_tiles(f"ln_{k}") for k in ("x", "t", "x1", "o", "y", "f")}
        hv = sb("ln_xx_var", [P, T])
        hd = sb("ln_xx_ve", [P, T])
        hr = sb("ln_xx_r", [P, T])

        bank_of = [ctx.enter_context(nc.psum_tensor(f"bank{i}", [P, N], f32)) for i in range(8)]
        BANKS = {"yT": 5, "h2u3": 6, "fT": 1, "p0": 2, "q0": 5, "p1": 3, "q1": 7, "q2": 2, "p2": 4, "s0": 6, "s1": 0,
                 "p3": 5, "q3": 4, "nT": 1, "t": 0, "h1u0": 5, "h1u1": 7, "h1_0": 6, "h1_1": 2, "h1_2": 3, "h1_3": 1,
                 "mT": 2, "h2_0": 0, "fmu0": 1, "fmu1": 2, "fmu2": 6, "h2_1": 5, "fmu3": 4, "fmd": 7, "h1u2": 3, "h1d": 4,
                 "oT": 1, "h2u0": 6, "h1u3": 2, "h2_2": 7, "h2_3": 1, "h2u1": 5, "h2u2": 3, "w3": 7, "h2d": 0}
        BANK_LEAD = {"yT": 0, "h2u3": 1, "fT": -1, "p0": 0, "q0": 0, "p1": 0, "q1": 0, "q2": 0, "p2": 0, "s0": 1, "s1": 1,
                     "p3": 0, "q3": 0, "nT": 2, "t": 1, "h1u0": 2, "h1u1": 2, "h1_0": 0, "h1_1": 0, "h1_2": 0, "h1_3": 0,
                     "mT": 1, "h2_0": 0, "fmu0": 1, "fmu1": 1, "fmu2": 1, "h2_1": 0, "fmu3": 1, "fmd": 1, "h1u2": 2,
                     "h1d": 2, "oT": 1, "h2u0": 2, "h1u3": 2, "h2_2": 0, "h2_3": 0, "h2u1": 2, "h2u2": 2, "w3": 0, "h2d":
                     2}

        def bank(group):
            return bank_of[BANKS[group]]

        x_first, x_rest = sem("x_first"), sem("x_rest")
        PIECES = [("a", 0, 2 * DI), ("a", 2 * DI, 4 * DI), ("a", 4 * DI, 6 * DI),
                  ("f", F_W1, F_H1), ("f", F_H1, F_H2), ("f", F_H2, F_H2 + 2 * DI), ("f", F_H2 + 2 * DI, F_H2 + J * DI)]
        w_in = [sem(f"w_in{k}") for k in range(len(PIECES))]
        consts_ready = sem("consts_ready")
        dve_consts = sem("dve_consts")
        split_hi, split_lo_a, split_lo_f = sem("split_hi"), sem("split_lo_a"), sem("split_lo_f")
        lo_summed, lo_tested, lo_counted, lo_flagged = (sem(s) for s in ("lo_summed", "lo_tested", "lo_counted", "lo_flagged"))
        stored = sem("stored")

        head_vector = Milestones(main=(sem("head_vector"), "stats aggr"))
        head_pool = Milestones(main=(sem("head_pool"), "ve r xm n0 vr v0 ve0 r0 n0g nr nf n0b1 n_lo"))
        head_scalar = Milestones(main=(sem("head_scalar"), "n_hi"))
        attn_tensor = Milestones(main=(sem("attn_tensor"), "h2u3 h2d s0 s1 t mT fmu0 fmu1 fmu2 fmu3 fmd oT"),
            early=(sem("attn_tensor_early"), "nT h1u0 h1u1 h1u2 h2u0 h1u3 h2u1 h1d h2u2"))
        attn_scalar = Milestones(main=(sem("attn_scalar"), "t mT_hi mT_g fm_hi0 fm_g0 fm_hi1 fm_g1 fm_hi2 fm_g2 fm_hi3 fm_g3 fm_out"),
            early=(sem("attn_scalar_early"), "h1_hi0 h1_g0 h1_hi1 h1_g1 h1_hi2 h1_g2 h1_hi3 h1_g3 h2_hi0 h2_g0 h2_hi1 h2_g1 h1T_hi h2_hi2 "
            "h2_g2 h2_hi3 h2_g3 h2T_hi s_hi0 s_hi1"),
            earlier=(sem("attn_scalar_earlier"), "nT_hi"))
        attn_vector = Milestones(main=(sem("attn_vector"), "mT_lo fm_lo0 fm_lo1 fm_lo2 fm_lo3 out o_stats o_aggr"),
            early=(sem("attn_vector_early"), "h1_lo0 h1_lo1 h1_lo2 h1_lo3 h2_lo0 h2_lo1 h1T_lo h2_lo2 h2_lo3 h2T_lo s_mask0 s_mask1 s_lo0 "
            "s_lo1 t_stats t_aggr t_g x1 x1_stats x1_aggr m"),
            earlier=(sem("attn_vector_earlier"), "nT_lo"))
        attn_pool = Milestones(main=(sem("attn_pool"), "o_ve o_r"),
            early=(sem("attn_pool_early"), "n0b2 t_ve t_r x1_ve x1_r"))
        ffn_tensor = Milestones(main=(sem("ffn_tensor"), "yT p0 q0 p1 q1 q2 p2 p3 q3 h1_0 h1_1 h1_2 h1_3 h2_0 h2_1 h2_2 h2_3 w3"))
        ffn_scalar = Milestones(main=(sem("ffn_scalar"), "g_hi3 h1_hi0 h1_g0 h1_hi1 h1_g1 h1_hi2 h1_g2 h1_hi3 h1_g3 h2_hi0 h2_g0 h2_hi1 h2_g1 h2_hi2 "
            "h2_g2 h2_hi3 h2_g3 w3"),
            early=(sem("ffn_scalar_early"), "yT_hi th0 th1 g_hi0 th2 g_hi1 th3 g_hi2"))
        ffn_vector = Milestones(main=(sem("ffn_vector"), "h1_lo2 h1_lo3 h2_lo0 h2_lo1 h2_lo2 h2_lo3"),
            early=(sem("ffn_vector_early"), "on y_stats y_aggr y yT_lo u0 g0 u1 g1 g_lo0 u2 g2 g_lo1 u3 g3 g_lo2 g_lo3 h1_lo0 h1_lo1"))
        ffn_pool = Milestones(main=(sem("ffn_pool"), "xo y_ve y_r"))
        end_tensor = Milestones(main=(sem("end_tensor"), "fT"))
        end_vector = Milestones(main=(sem("end_vector"), "f_stats f_aggr"))
        end_pool = Milestones(main=(sem("end_pool"), "f_ve f_r f_mr f_nmr xf"))
        end_scalar = Milestones(main=(sem("end_scalar"), "fn"))
        READ_BY = {"nT": (attn_vector, "nT_lo"), "mT": (attn_vector, "mT_lo"), "oT": (attn_vector, "out"),
                   "h1d": (attn_vector, "h1T_lo"), "h2d": (attn_vector, "h2T_lo"), "fmd": (attn_scalar, "fm_out"),
                   "s0": (attn_vector, "s_lo0"), "s1": (attn_vector, "s_lo1"), "t": (attn_vector, "t_g"),
                   "yT": (ffn_vector, "yT_lo"), "w3": (ffn_scalar, "w3"), "fT": (end_scalar, "fn")}
        for j in range(J):
            READ_BY |= {f"{L}u{j}": (attn_vector, f"{L}_lo{j}") for L in ("h1", "h2", "fm")}
            READ_BY |= {f"p{j}": (ffn_vector, f"u{j}"), f"q{j}": (ffn_vector, f"g_lo{j}"),
                        f"h1_{j}": (ffn_vector, f"h1_lo{j}"), f"h2_{j}": (ffn_vector, f"h2_lo{j}")}
        first_head, first_scaled = sem("first_head"), sem("first_scaled")
        params_in = sem("params_in")
        dve_waited, pool_waited = sem("dve_waited"), sem("pool_waited")

        def piece_dst(k, half):
            kind, c0, c1 = PIECES[k]
            return (Aw if kind == "a" else Fw)[half][:, c0:c1]

        def piece_raw(k):
            kind, c0, c1 = PIECES[k]
            if kind == "a":
                return raw_a[:, c0:c1]
            return [raw_b[:, 0:3 * DI], raw_a[:, 0:4 * DI], raw_a[:, 4 * DI:6 * DI], raw_b[:, 0:2 * DI]][k - 3]

        def flat(ap):
            return ap.rearrange("p t d -> p (t d)")

        LEADS = {"tensor": (-1, 2), "scalar": (-1, 2), "vector": (-1, 2), "pool": (-1, 2)}

        def on(chunk, step, *args):
            if not isinstance(chunk, int) or 0 <= chunk < CHUNKS:
                step(*args, chunk)

        def once(chunk, step):
            if isinstance(chunk, int) and chunk == 0:
                step()

        def iterations(engine, iteration, leads, first=None):
            low, high = leads
            for i in range(-high if first is None else first, -low):
                iteration(i)
            with engine.Fori(-low, CHUNKS - high) as i:
                iteration(i)
            for i in range(CHUNKS - high, CHUNKS - low):
                iteration(i)

        def row(r):
            return bc[:, r:r + 1, :].broadcast_to([P, T, D])

        block = ctx.enter_context(nc.Block())

        @block.sync
        def _(sp):
            xv = x.rearrange("b (s p) d -> p (b s) d", p=P)
            ov = out.rearrange("b (s p) d -> p (b s) d", p=P)
            sp.dma_start(X[:, 0:T, :], xv[:, 0:T, :]).then_inc(x_first, 16)
            sp.dma_start(bc[:, :, :], rows.rearrange("(o r) d -> o r d", o=1).broadcast_to([P, 3, D])).then_inc(params_in, 16)
            sp.dma_start(cols[:, :], columns).then_inc(params_in, 16)
            sp.dma_start(piece_raw(0), attn_w[:, 0:2 * DI]).then_inc(w_in[0], 16)
            sp.dma_start(piece_raw(1), attn_w[:, 2 * DI:4 * DI]).then_inc(w_in[1], 16)
            sp.dma_start(piece_raw(2), attn_w[:, 4 * DI:6 * DI]).then_inc(w_in[2], 16)
            sp.dma_start(piece_raw(3), ffn_w[:, F_W1:F_H1]).then_inc(w_in[3], 16)
            sp.dma_start(X[:, T:TILES, :], xv[:, T:TILES, :]).then_inc(x_rest, 16)
            for k in range(4, len(PIECES)):
                sp.wait_ge(split_hi, 4 if k == 6 else 3)
                if k == 6:
                    sp.wait_ge(split_lo_f, 1)
                else:
                    sp.wait_ge(split_lo_a, 3)
                _, c0, c1 = PIECES[k]
                sp.dma_start(piece_raw(k), ffn_w[:, c0:c1]).then_inc(w_in[k], 16)
            for c in range(CHUNKS):
                sp.wait_ge(end_pool.sem("xf"), end_pool.after("xf", c))
                sp.dma_start(ov[:, c * T:(c + 1) * T, :], X[:, c * T:(c + 1) * T, :]).then_inc(stored, 16)
            sp.wait_ge(stored, 16 * CHUNKS)

        @block.gpsimd
        def _(pool):
            for steps in (head_pool, attn_pool, ffn_pool, end_pool):
                steps.start(nc.gpsimd)
            nc.gpsimd.memset(eps[:, :], EPS)
            nc.gpsimd.memset(neg_half[:, :], -0.5)
            nc.gpsimd.memset(zeros[:, :], 0.0)
            nc.gpsimd.memset(ones[:, :], 1.0)
            nc.gpsimd.memset(ident[:, :], 0.0)
            nc.gpsimd.memset(mask[:, :, :], 1.0).then_inc(consts_ready, 1)
            pool.wait_ge(consts_ready, 1)
            nc.gpsimd.affine_select(out=ident[:, :], in_=ident[:, :], compare_op=ALU.not_equal, fill=1.0,
                                    base=0, pattern=[[-1, P]], channel_multiplier=1).then_inc(consts_ready, 1)
            for k in (0, 1):
                nc.gpsimd.affine_select(out=mask[:, k, :], in_=mask[:, k, :], compare_op=ALU.is_ge, fill=0.0,
                                        base=0, pattern=[[1, P]], channel_multiplier=-1).then_inc(consts_ready, 1)

            def rstd(ms, name, ln, aggr_sem, aggr_value, chunk):
                pool.wait_ge(aggr_sem, aggr_value)
                nc.gpsimd.tensor_tensor(ln["ve"][:, :], ln["mv"][:, :, 1], eps[:, :], ALU.add).then_inc(ms.sem(f"{name}ve"), ms.step(f"{name}ve"))
                pool.wait_ge(ms.sem(f"{name}ve"), ms.after(f"{name}ve", chunk))
                nc.gpsimd.tensor_tensor(ln["r"][:, :], ln["ve"][:, :], neg_half[:, :], ALU.pow).then_inc(ms.sem(f"{name}r"), ms.step(f"{name}r"))

            def head_rstd(c):
                rstd(head_pool, "", LN["x"], head_vector.sem("aggr"), head_vector.after("aggr", c), c)

            def head_rstd2(c):
                ms = head_pool
                pool.wait_ge(ms.sem("r"), ms.after("r", c))
                nc.gpsimd.tensor_tensor(hv[:, :], LN["x"]["mv"][:, :, 1], LN["x"]["r"][:, :], ALU.mult).then_inc(ms.sem("vr"), ms.step("vr"))
                pool.wait_ge(ms.sem("vr"), ms.after("vr", c))
                nc.gpsimd.tensor_tensor(hd[:, :], hv[:, :], LN["x"]["r"][:, :], ALU.mult).then_inc(ms.sem("v0"), ms.step("v0"))
                pool.wait_ge(ms.sem("v0"), ms.after("v0", c))
                nc.gpsimd.tensor_tensor(hv[:, :], hd[:, :], eps[:, :], ALU.add).then_inc(ms.sem("ve0"), ms.step("ve0"))
                pool.wait_ge(ms.sem("ve0"), ms.after("ve0", c))
                nc.gpsimd.tensor_tensor(hr[:, :], hv[:, :], neg_half[:, :], ALU.pow).then_inc(ms.sem("r0"), ms.step("r0"))

            def by_vector(ms, value, *steps):
                pool.wait_ge(first_head, value)
                for step in steps:
                    pool.wait_ge(ms.sem(step), ms.after(step, 0) - 1)
                    nc.gpsimd.sem_inc(ms.sem(step), ms.step(step))

            def head_n0(c):
                ms, ln = head_pool, LN["x"]
                if isinstance(c, int) and c == 0:
                    return by_vector(ms, 1, "xm", "n0")
                pool.wait_ge(ms.sem("r"), ms.after("r", c))
                pool.wait_ge(attn_pool.sem("n0b2"), attn_pool.after("n0b2", c - 1))
                nc.gpsimd.sem_inc(pool_waited, 1)
                nc.gpsimd.tensor_tensor(N0[:, :, :], X[:, bass.ds(c * T, T), :], ln["mv"][:, :, 0:1].broadcast_to([P, T, D]),
                                        ALU.subtract).then_inc(ms.sem("xm"), ms.step("xm"))
                pool.wait_ge(ms.sem("xm"), ms.after("xm", c))
                nc.gpsimd.tensor_tensor(N0[:, :, :], N0[:, :, :], ln["r"].rearrange("p (t o) -> p t o", o=1).broadcast_to([P, T, D]),
                                        ALU.mult).then_inc(ms.sem("n0"), ms.step("n0"))

            def head_scaled(c):
                ms = head_pool
                pool.wait_ge(attn_tensor.sem("nT"), attn_tensor.after("nT", c - 1))
                pool.wait_ge(ms.sem("n_lo"), ms.after("n_lo", c - 1))
                if isinstance(c, int) and c == 0:
                    return by_vector(ms, 1, "n0g")
                pool.wait_ge(head_pool.sem("n0"), head_pool.after("n0", c))
                nc.gpsimd.tensor_tensor(NF[:, :, :], N0[:, :, :], row(R_G), ALU.mult).then_inc(ms.sem("n0g"), ms.step("n0g"))

            def head_shifted(c):
                ms = head_pool
                if isinstance(c, int) and c == 0:
                    pool.wait_ge(params_in, 32)
                pool.wait_ge(head_pool.sem("n0"), head_pool.after("n0", c))
                pool.wait_ge(attn_vector.sem("x1"), attn_vector.after("x1", c - 1))
                nc.gpsimd.tensor_tensor(N0B1[:, :, :], N0[:, :, :], row(R_B), ALU.add).then_inc(ms.sem("n0b1"), ms.step("n0b1"))

            def head_n(c):
                ms = head_pool
                if isinstance(c, int) and c == 0:
                    return by_vector(ms, 2, "nr", "nf")
                pool.wait_ge(ms.sem("n0g"), ms.after("n0g", c))
                pool.wait_ge(ms.sem("r0"), ms.after("r0", c))
                nc.gpsimd.tensor_tensor(NF[:, :, :], NF[:, :, :], hr.rearrange("p (t o) -> p t o", o=1).broadcast_to([P, T, D]),
                                        ALU.mult).then_inc(ms.sem("nr"), ms.step("nr"))
                pool.wait_ge(ms.sem("nr"), ms.after("nr", c))
                nc.gpsimd.tensor_tensor(NF[:, :, :], NF[:, :, :], row(R_B), ALU.add).then_inc(ms.sem("nf"), ms.step("nf"))

            def head_low(c):
                ms = head_pool
                pool.wait_ge(head_scalar.sem("n_hi"), head_scalar.after("n_hi", c))
                nc.gpsimd.tensor_tensor(n_tok[1][:, :, :], NF[:, :, :], n_tok[0][:, :, :].bitcast(f32), ALU.subtract)\
                    .then_inc(ms.sem("n_lo"), ms.step("n_lo"))

            def x_after_attention(f):
                pool.wait_ge(ffn_vector.sem("on"), ffn_vector.after("on", f))
                nc.gpsimd.sem_inc(pool_waited, 1)
                xc = X[:, bass.ds(f * T, T), :]
                nc.gpsimd.tensor_tensor(xc, xc, X1[:, :, :], ALU.add).then_inc(ffn_pool.sem("xo"), ffn_pool.step("xo"))

            def residual_b2(a):
                pool.wait_ge(head_pool.sem("n0"), head_pool.after("n0", a))
                pool.wait_ge(attn_vector.sem("out"), attn_vector.after("out", a - 1))
                nc.gpsimd.tensor_tensor(N0B2[:, :, :], N0[:, :, :], row(R_B2), ALU.add).then_inc(attn_pool.sem("n0b2"), attn_pool.step("n0b2"))

            def attn_rstd(name, a):
                rstd(attn_pool, f"{name}_", LN[name], attn_vector.sem(f"{name}_aggr"), attn_vector.after(f"{name}_aggr", a), a)

            def y_rstd(f):
                rstd(ffn_pool, "y_", LN["y"], ffn_vector.sem("y_aggr"), ffn_vector.after("y_aggr", f), f)

            def end_rstd(e):
                ms, ln = end_pool, LN["f"]
                rstd(ms, "f_", ln, end_vector.sem("f_aggr"), end_vector.after("f_aggr", e), e)
                pool.wait_ge(ms.sem("f_r"), ms.after("f_r", e))
                nc.gpsimd.tensor_tensor(ln["ve"][:, :], ln["mv"][:, :, 0], ln["r"][:, :], ALU.mult).then_inc(ms.sem("f_mr"), ms.step("f_mr"))
                pool.wait_ge(ms.sem("f_mr"), ms.after("f_mr", e))
                nc.gpsimd.tensor_tensor(ln["nmr"][:, :], zeros[:, :], ln["ve"][:, :], ALU.subtract).then_inc(ms.sem("f_nmr"), ms.step("f_nmr"))

            def end_sum(e):
                pool.wait_ge(end_scalar.sem("fn"), end_scalar.after("fn", e))
                nc.gpsimd.sem_inc(pool_waited, 1)
                xc = X[:, bass.ds(e * T, T), :]
                nc.gpsimd.tensor_tensor(xc, xc, FN[:, :, :], ALU.add).then_inc(end_pool.sem("xf"), end_pool.step("xf"))

            def iteration(i):
                on(i, attn_rstd, "o")
                on(i + 1, residual_b2)
                on(i, x_after_attention)
                on(i, y_rstd)
                on(i + 2, head_rstd)
                on(i + 2, head_n0)
                on(i + 2, head_rstd2)
                on(i - 1, end_rstd)
                on(i + 2, head_scaled)
                on(i + 2, head_n)
                on(i + 1, attn_rstd, "t")
                on(i + 2, head_shifted)
                on(i + 1, attn_rstd, "x1")
                on(i - 1, end_sum)
                on(i + 2, head_low)

            iterations(pool, iteration, LEADS["pool"])

        @block.scalar
        def _(act):
            for steps in (head_scalar, attn_scalar, ffn_scalar, end_scalar):
                steps.start(nc.scalar)
            act.wait_ge(consts_ready, 1)
            nc.scalar.activation(warm[:, :], ones[:, :], ACT.Gelu)
            for k in range(4):
                act.wait_ge(w_in[k], 16)
                nc.scalar.activation(piece_dst(k, 0), piece_raw(k), ACT.Copy).then_inc(split_hi, 1)
            act.wait_ge(params_in, 32)

            def head(c):
                act.wait_ge(attn_tensor.sem("t"), attn_tensor.after("t", c - 1))
                act.wait_ge(head_pool.sem("nf"), head_pool.after("nf", c))
                nc.scalar.activation(n_tok[0][:, :, :], NF[:, :, :], ACT.Copy).then_inc(head_scalar.sem("n_hi"), head_scalar.step("n_hi"))

            def hi_copy(ms, name, tensor, group, dst, chunk):
                act.wait_ge(tensor.sem(group), tensor.after(group, chunk))
                nc.scalar.activation(dst, bank(group)[:, :], ACT.Copy).then_inc(ms.sem(name), ms.step(name))

            def gelu(ms, L, j, tensor, group, dst, chunk, **affine):
                act.wait_ge(tensor.sem(group), tensor.after(group, chunk))
                nc.scalar.activation(dst, bank(group)[:, :], ACT.Gelu, **affine).then_inc(ms.sem(f"{L}_hi{j}"), ms.step(f"{L}_hi{j}"))
                act.wait_ge(ms.sem(f"{L}_hi{j}"), ms.after(f"{L}_hi{j}", chunk))
                nc.scalar.activation(bank(group)[:, :], bank(group)[:, :], ACT.Gelu, **affine).then_inc(ms.sem(f"{L}_g{j}"), ms.step(f"{L}_g{j}"))

            def up(L, j, a):
                slot = (SLOT0[L] + j) % SLOTS
                gelu(attn_scalar, L, j, attn_tensor, f"{L}u{j}", HA[0][:, slot, :], a,
                     bias=cols[:, C_B1[L] + j:C_B1[L] + j + 1])

            def down(L, a):
                act.wait_ge(attn_tensor.sem(f"{L}d"), attn_tensor.after(f"{L}d", a))
                nc.scalar.activation(WT[L][0][:, :], bank(f"{L}d")[:, :], ACT.Identity,
                                     bias=cols[:, C_B2[L]:C_B2[L] + 1]).then_inc(attn_scalar.sem(f"{L}T_hi"), attn_scalar.step(f"{L}T_hi"))

            def scores(b, a):
                act.wait_ge(attn_vector.sem(f"s_mask{b}"), attn_vector.after(f"s_mask{b}", a))
                nc.scalar.activation(flat(SC[0][:, b, :, :]), bank(f"s{b}")[:, 0:3 * P], ACT.Copy)\
                    .then_inc(attn_scalar.sem(f"s_hi{b}"), attn_scalar.step(f"s_hi{b}"))

            def t_gelu(a):
                act.wait_ge(attn_tensor.sem("t"), attn_tensor.after("t", a))
                nc.scalar.activation(bank("t")[:, :], bank("t")[:, :], ACT.Gelu).then_inc(attn_scalar.sem("t"), attn_scalar.step("t"))

            def m_transposed(a):
                if isinstance(a, int) and a == 0:
                    act.wait_ge(lo_summed, 4)
                act.wait_ge(attn_tensor.sem("mT"), attn_tensor.after("mT", a))
                g, b = cols[:, C_G:C_G + 1], cols[:, C_B:C_B + 1]
                nc.scalar.activation(mT[0][:, :], bank("mT")[:, :], ACT.Identity, scale=g, bias=b)\
                    .then_inc(attn_scalar.sem("mT_hi"), attn_scalar.step("mT_hi"))
                act.wait_ge(attn_scalar.sem("mT_hi"), attn_scalar.after("mT_hi", a))
                nc.scalar.activation(bank("mT")[:, :], bank("mT")[:, :], ACT.Identity, scale=g, bias=b)\
                    .then_inc(attn_scalar.sem("mT_g"), attn_scalar.step("mT_g"))

            def tanh(j, f):
                if j:
                    act.wait_ge(ffn_vector.sem(f"g{j - 1}"), ffn_vector.after(f"g{j - 1}", f))
                act.wait_ge(ffn_tensor.sem(f"p{j}"), ffn_tensor.after(f"p{j}", f))
                nc.scalar.activation(TH[:, :], bank(f"p{j}")[:, :], ACT.Tanh, scale=gate_half[:, j:j + 1])\
                    .then_inc(ffn_scalar.sem(f"th{j}"), ffn_scalar.step(f"th{j}"))

            def gate_hi(j, f):
                act.wait_ge(ffn_vector.sem(f"g{j}"), ffn_vector.after(f"g{j}", f))
                nc.scalar.activation(HG[0][:, j, :], bank(f"q{j}")[:, :], ACT.Copy)\
                    .then_inc(ffn_scalar.sem(f"g_hi{j}"), ffn_scalar.step(f"g_hi{j}"))

            def layer(L, j, f):
                dst = HF if L == "h1" else HG
                gelu(ffn_scalar, L, j, ffn_tensor, f"{L}_{j}", dst[0][:, j, :], f,
                     scale=cols[:, C_HS[L] + j:C_HS[L] + j + 1])

            def n_transposed(a):
                hi_copy(attn_scalar, "nT_hi", attn_tensor, "nT", aT[0][:, :], a)

            def y_transposed(f):
                hi_copy(ffn_scalar, "yT_hi", ffn_tensor, "yT", yT[0][:, :], f)

            def fm_out(a):
                act.wait_ge(attn_tensor.sem("fmd"), attn_tensor.after("fmd", a))
                nc.scalar.activation(OTA[:, :], bank("fmd")[:, :], ACT.Copy).then_inc(attn_scalar.sem("fm_out"), attn_scalar.step("fm_out"))

            def w3_out(f):
                act.wait_ge(end_tensor.sem("fT"), end_tensor.after("fT", f - 1))
                act.wait_ge(ffn_tensor.sem("w3"), ffn_tensor.after("w3", f))
                nc.scalar.activation(OTF[:, :], bank("w3")[:, :], ACT.Copy, scale=cols[:, C_S3:C_S3 + 1])\
                    .then_inc(ffn_scalar.sem("w3"), ffn_scalar.step("w3"))

            def end_normalise(e):
                act.wait_ge(end_pool.sem("xf"), end_pool.after("xf", e - 1))
                act.wait_ge(end_pool.sem("f_nmr"), end_pool.after("f_nmr", e))
                for t in range(T):
                    last = nc.scalar.activation(FN[:, t, :], bank("fT")[:, t * P:(t + 1) * P], ACT.Identity,
                                                scale=LN["f"]["r"][:, t:t + 1], bias=LN["f"]["nmr"][:, t:t + 1])
                last.then_inc(end_scalar.sem("fn"), end_scalar.step("fn"))

            def split_weights(k):
                act.wait_ge(w_in[k], 16)
                nc.scalar.activation(piece_dst(k, 0), piece_raw(k), ACT.Copy).then_inc(split_hi, 1)

            def sum_low_parts():
                for k in range(3, len(PIECES)):
                    act.wait_ge(split_lo_f, max(k, 4) - 2)
                    if k == 4:
                        act.wait_ge(lo_summed, 1)
                    terms = raw_a[:, 0:3 * DI] if k == 3 else piece_raw(k)
                    nc.scalar.activation(terms, piece_dst(k, 1).bitcast(f32), ACT.Abs,
                                         accum_out=lo_sum[:, k - 3:k - 2]).then_inc(lo_summed, 1)

            def iteration(i):
                on(i, t_gelu)
                once(i, sum_low_parts)
                on(i - 1, gate_hi, 3)
                on(i + 1, head)
                on(i + 1, up, "h1", 0)
                on(i + 1, up, "h1", 1)
                on(i - 1, layer, "h1", 0)
                on(i - 1, layer, "h1", 1)
                on(i - 1, layer, "h1", 2)
                on(i - 1, layer, "h1", 3)
                on(i, m_transposed)
                on(i, up, "fm", 0)
                on(i, up, "fm", 1)
                on(i, up, "fm", 2)
                on(i, up, "fm", 3)
                on(i - 1, layer, "h2", 0)
                on(i, fm_out)
                on(i + 1, up, "h1", 2)
                on(i - 1, layer, "h2", 1)
                on(i + 1, up, "h1", 3)
                on(i - 1, layer, "h2", 2)
                on(i + 1, up, "h2", 0)
                on(i - 1, layer, "h2", 3)
                on(i + 1, up, "h2", 1)
                on(i + 1, down, "h1")
                on(i + 1, up, "h2", 2)
                on(i - 1, w3_out)
                on(i, y_transposed)
                on(i + 1, up, "h2", 3)
                on(i, tanh, 0)
                on(i + 1, down, "h2")
                on(i, tanh, 1)
                on(i, gate_hi, 0)
                on(i - 1, end_normalise)
                on(i, tanh, 2)
                on(i + 1, scores, 0)
                on(i + 1, scores, 1)
                once(i + 1, lambda: split_weights(4))
                once(i + 1, lambda: split_weights(5))
                once(i + 1, lambda: split_weights(6))
                on(i, gate_hi, 1)
                on(i, tanh, 3)
                on(i, gate_hi, 2)
                on(i + 2, n_transposed)

            iterations(act, iteration, LEADS["scalar"])

        @block.vector
        def _(dve):
            def alone():
                nc.vector.sem_inc(dve_waited, 1)

            def stats(ms, name, src, ln, chunk):
                for t in range(T):
                    last = nc.vector.bn_stats(ln["st"][:, t, :], src(t))
                last.then_inc(ms.sem(f"{name}stats"), ms.step(f"{name}stats"))
                dve.wait_ge(ms.sem(f"{name}stats"), ms.after(f"{name}stats", chunk))
                alone()
                for t in range(T):
                    last = nc.vector.bn_aggr(ln["mv"][:, t, :], ln["st"][:, t, :])
                last.then_inc(ms.sem(f"{name}aggr"), ms.step(f"{name}aggr"))

            def normalise(ms, name, dst, src, ln):
                for t in range(T):
                    last = nc.vector.tensor_scalar(dst(t), src(t), ln["mv"][:, t, 0:1], ln["r"][:, t:t + 1],
                                                   ALU.subtract, ALU.mult)
                last.then_inc(ms.sem(name), ms.step(name))

            def x_tile(c):
                return lambda t: X[:, c * T + t, :]

            def tile_of(buf):
                return lambda t: buf[:, t, :]

            def low(ms, name, dst, whole, high):
                nc.vector.tensor_tensor(dst, whole, high.bitcast(f32), ALU.subtract).then_inc(ms.sem(name), ms.step(name))

            def head_stats(c):
                if isinstance(c, int) and c < 2:
                    dve.wait_ge((x_first, x_rest)[c], 16)
                    alone()
                dve.wait_ge(head_pool.sem("r0"), head_pool.after("r0", c - 1))
                dve.wait_ge(head_pool.sem("n0b1"), head_pool.after("n0b1", c - 1))
                alone()
                stats(head_vector, "", x_tile(c), LN["x"], c)

            def attn_low(name, scalar_step, dst, group, high, a):
                dve.wait_ge(attn_scalar.sem(scalar_step), attn_scalar.after(scalar_step, a))
                low(attn_vector, name, dst, bank(group)[:, :], high)

            def up_low(L, j, a):
                slot = (SLOT0[L] + j) % SLOTS
                attn_low(f"{L}_lo{j}", f"{L}_g{j}", HA[1][:, slot, :], f"{L}u{j}", HA[0][:, slot, :], a)

            def down_low(L, a):
                dve.wait_ge(attn_scalar.sem(f"{L}T_hi"), attn_scalar.after(f"{L}T_hi", a))
                nc.vector.scalar_tensor_tensor(WT[L][1][:, :], bank(f"{L}d")[:, :], cols[:, C_B2[L]:C_B2[L] + 1],
                                               WT[L][0][:, :].bitcast(f32), ALU.add, ALU.subtract)\
                    .then_inc(attn_vector.sem(f"{L}T_lo"), attn_vector.step(f"{L}T_lo"))

            def score_mask(b, a):
                dve.wait_ge(attn_tensor.sem(f"s{b}"), attn_tensor.after(f"s{b}", a))
                diagonal = bank(f"s{b}")[:, 0:4 * P].rearrange("p (k z) -> p k z", k=4)[:, 0:3:2, :]
                nc.vector.tensor_tensor(diagonal, diagonal, mask[:, :, :], ALU.mult)\
                    .then_inc(attn_vector.sem(f"s_mask{b}"), attn_vector.step(f"s_mask{b}"))

            def score_low(b, a):
                dve.wait_ge(attn_scalar.sem(f"s_hi{b}"), attn_scalar.after(f"s_hi{b}", a))
                low(attn_vector, f"s_lo{b}", flat(SC[1][:, b, :, :]), bank(f"s{b}")[:, 0:3 * P], flat(SC[0][:, b, :, :]))

            tb = bank("t")[:, :].rearrange("p (t d) -> p t d", t=T)

            def t_stats(a):
                ms = attn_vector
                dve.wait_ge(attn_scalar.sem("t"), attn_scalar.after("t", a))
                alone()
                stats(ms, "t_", tile_of(tb), LN["t"], a)

            def t_scaled(a):
                ms = attn_vector
                dve.wait_ge(ffn_pool.sem("xo"), ffn_pool.after("xo", a - 1))
                dve.wait_ge(ms.sem("t_aggr"), ms.after("t_aggr", a))
                for t in range(T):
                    last = nc.vector.scalar_tensor_tensor(X1[:, t, :], tb[:, t, :], LN["t"]["mv"][:, t, 0:1],
                                                          bc[:, R_G, :], ALU.subtract, ALU.mult)
                last.then_inc(ms.sem("t_g"), ms.step("t_g"))

            def x1_sum(a):
                ms = attn_vector
                dve.wait_ge(head_pool.sem("n0b1"), head_pool.after("n0b1", a))
                dve.wait_ge(attn_pool.sem("t_r"), attn_pool.after("t_r", a))
                dve.wait_ge(ms.sem("t_g"), ms.after("t_g", a))
                for t in range(T):
                    last = nc.vector.scalar_tensor_tensor(X1[:, t, :], X1[:, t, :], LN["t"]["r"][:, t:t + 1],
                                                          N0B1[:, t, :], ALU.mult, ALU.add)
                last.then_inc(ms.sem("x1"), ms.step("x1"))

            def x1_stats(a):
                ms = attn_vector
                dve.wait_ge(ms.sem("x1"), ms.after("x1", a))
                alone()
                stats(ms, "x1_", tile_of(X1), LN["x1"], a)

            def m_norm(a):
                dve.wait_ge(attn_pool.sem("x1_r"), attn_pool.after("x1_r", a))
                normalise(attn_vector, "m", tile_of(X1), tile_of(X1), LN["x1"])

            def branch_out(a):
                ms = attn_vector
                dve.wait_ge(attn_pool.sem("n0b2"), attn_pool.after("n0b2", a))
                dve.wait_ge(attn_tensor.sem("oT"), attn_tensor.after("oT", a))
                nc.vector.tensor_tensor(flat(X1[:, :, :]), bank("oT")[:, :], flat(N0B2[:, :, :]), ALU.add)\
                    .then_inc(ms.sem("out"), ms.step("out"))

            def branch_stats(a):
                ms = attn_vector
                dve.wait_ge(ms.sem("out"), ms.after("out", a))
                alone()
                stats(ms, "o_", tile_of(X1), LN["o"], a)

            def branch_norm(f):
                ms = ffn_vector
                dve.wait_ge(attn_pool.sem("o_r"), attn_pool.after("o_r", f))
                normalise(ms, "on", tile_of(X1), tile_of(X1), LN["o"])

            def y_stats(f):
                dve.wait_ge(ffn_pool.sem("xo"), ffn_pool.after("xo", f))
                alone()
                stats(ffn_vector, "y_", x_tile(f), LN["y"], f)

            def y_norm(f):
                dve.wait_ge(ffn_pool.sem("y_r"), ffn_pool.after("y_r", f))
                normalise(ffn_vector, "y", tile_of(YF), x_tile(f), LN["y"])

            def gate(j, f):
                ms = ffn_vector
                dve.wait_ge(ffn_tensor.sem(f"q{j}"), ffn_tensor.after(f"q{j}", f))
                dve.wait_ge(ffn_scalar.sem(f"th{j}"), ffn_scalar.after(f"th{j}", f))
                nc.vector.scalar_tensor_tensor(TH[:, :], TH[:, :], 1.0, bank(f"p{j}")[:, :], ALU.add, ALU.mult)\
                    .then_inc(ms.sem(f"u{j}"), ms.step(f"u{j}"))
                dve.wait_ge(ms.sem(f"u{j}"), ms.after(f"u{j}", f))
                nc.vector.scalar_tensor_tensor(bank(f"q{j}")[:, :], TH[:, :], gate_coef[:, j:j + 1], bank(f"q{j}")[:, :],
                                               ALU.mult, ALU.mult).then_inc(ms.sem(f"g{j}"), ms.step(f"g{j}"))

            def gate_low(j, f):
                dve.wait_ge(ffn_scalar.sem(f"g_hi{j}"), ffn_scalar.after(f"g_hi{j}", f))
                low(ffn_vector, f"g_lo{j}", HG[1][:, j, :], bank(f"q{j}")[:, :], HG[0][:, j, :])

            def layer_low(L, j, f):
                buf = HF if L == "h1" else HG
                dve.wait_ge(ffn_scalar.sem(f"{L}_g{j}"), ffn_scalar.after(f"{L}_g{j}", f))
                low(ffn_vector, f"{L}_lo{j}", buf[1][:, j, :], bank(f"{L}_{j}")[:, :], buf[0][:, j, :])

            def y_low(f):
                dve.wait_ge(ffn_scalar.sem("yT_hi"), ffn_scalar.after("yT_hi", f))
                low(ffn_vector, "yT_lo", yT[1][:, :], bank("yT")[:, :], yT[0][:, :])

            def end_stats(e):
                dve.wait_ge(end_scalar.sem("fn"), end_scalar.after("fn", e - 1))
                alone()
                dve.wait_ge(end_tensor.sem("fT"), end_tensor.after("fT", e))
                alone()
                fT = bank("fT")[:, :].rearrange("p (t d) -> p t d", t=T)
                stats(end_vector, "f_", tile_of(fT), LN["f"], e)

            def split_weights(k):
                dve.wait_ge(split_hi, k + 1)
                nc.vector.tensor_tensor(piece_dst(k, 1), piece_raw(k), piece_dst(k, 0).bitcast(f32), ALU.subtract)\
                    .then_inc(split_lo_a if k < 3 else split_lo_f, 1)

            def first_n0():
                dve.wait_ge(head_pool.sem("r"), head_pool.after("r", 0))
                for t in range(T):
                    last = nc.vector.tensor_scalar(N0[:, t, :], X[:, t, :], LN["x"]["mv"][:, t, 0:1], LN["x"]["r"][:, t:t + 1],
                                                   ALU.subtract, ALU.mult)
                last.then_inc(first_head, 1)

            def first_n():
                dve.wait_ge(head_pool.sem("r0"), head_pool.after("r0", 0))
                dve.wait_ge(first_head, 1)
                for t in range(T):
                    last = nc.vector.scalar_tensor_tensor(NF[:, t, :], N0[:, t, :], hr[:, t:t + 1], bc[:, R_G, :],
                                                          ALU.mult, ALU.mult)
                last.then_inc(first_scaled, 1)
                dve.wait_ge(first_scaled, 1)
                nc.vector.tensor_tensor(NF[:, :, :], NF[:, :, :], row(R_B), ALU.add).then_inc(first_head, 1)

            def gate_constants():
                dve.wait_ge(params_in, 32)
                nc.vector.tensor_scalar(gate_half[:, :], cols[:, C_S1:C_S1 + J], 0.5, None, ALU.mult).then_inc(dve_consts, 1)
                dve.wait_ge(dve_consts, 1)
                nc.vector.tensor_tensor(gate_coef[:, :], gate_half[:, :], cols[:, C_S2:C_S2 + J], ALU.mult).then_inc(dve_consts, 1)
                dve.wait_ge(dve_consts, 2)
                dve.wait_ge(consts_ready, 4)
                alone()

            def flag_low_parts():
                dve.wait_ge(lo_summed, 4)
                nc.vector.tensor_scalar(lo_any[:, :], lo_sum[:, :], 0.0, None, ALU.not_equal).then_inc(lo_tested, 1)
                dve.wait_ge(lo_counted, 1)
                nc.vector.tensor_reduce(lo_flag[0:1, 0:1], bank("fmu0")[0:1, 0:4], mybir.AxisListType.X, ALU.add)\
                    .then_inc(lo_flagged, 1)

            for steps in (head_vector, attn_vector, ffn_vector, end_vector):
                steps.start(nc.vector)

            def iteration(i):
                on(i - 1, layer_low, "h1", 2)
                on(i - 1, layer_low, "h1", 3)
                once(i, flag_low_parts)
                on(i, attn_low, "mT_lo", "mT_g", mT[1][:, :], "mT", mT[0][:, :])
                on(i + 1, up_low, "h1", 0)
                on(i + 2, head_stats)
                once(i + 2, gate_constants)
                once(i + 2, first_n0)
                once(i + 2, lambda: split_weights(0))
                once(i + 2, first_n)
                once(i + 2, lambda: split_weights(1))
                once(i + 2, lambda: split_weights(2))
                on(i + 1, up_low, "h1", 1)
                on(i, up_low, "fm", 0)
                on(i, up_low, "fm", 1)
                on(i, up_low, "fm", 2)
                on(i, up_low, "fm", 3)
                on(i - 1, layer_low, "h2", 0)
                on(i, branch_out)
                on(i, branch_stats)
                on(i - 1, layer_low, "h2", 1)
                on(i + 1, up_low, "h1", 2)
                on(i, branch_norm)
                on(i - 1, layer_low, "h2", 2)
                on(i + 1, up_low, "h1", 3)
                on(i, y_stats)
                on(i - 1, layer_low, "h2", 3)
                on(i + 1, up_low, "h2", 0)
                on(i + 1, up_low, "h2", 1)
                on(i, y_norm)
                on(i + 1, down_low, "h1")
                on(i + 1, up_low, "h2", 2)
                on(i, y_low)
                on(i - 1, end_stats)
                on(i + 1, up_low, "h2", 3)
                on(i, gate, 0)
                on(i + 1, down_low, "h2")
                on(i, gate, 1)
                on(i + 1, score_mask, 0)
                on(i, gate_low, 0)
                on(i + 1, score_mask, 1)
                on(i, gate, 2)
                on(i + 1, score_low, 0)
                on(i + 1, score_low, 1)
                once(i + 1, lambda: split_weights(4))
                on(i, gate_low, 1)
                on(i, gate, 3)
                on(i + 2, attn_low, "nT_lo", "nT_hi", aT[1][:, :], "nT", aT[0][:, :])
                once(i + 2, lambda: split_weights(3))
                on(i, gate_low, 2)
                on(i + 1, t_stats)
                on(i, gate_low, 3)
                on(i + 1, t_scaled)
                once(i + 1, lambda: split_weights(5))
                on(i + 1, x1_sum)
                on(i + 1, x1_stats)
                once(i + 1, lambda: split_weights(6))
                on(i, layer_low, "h1", 0)
                on(i, layer_low, "h1", 1)
                on(i + 1, m_norm)

            iterations(dve, iteration, LEADS["vector"])

        @block.tensor
        def _(pe):
            for steps in (attn_tensor, ffn_tensor, end_tensor):
                steps.start(nc.tensor)

            def bank_free(group, chunk):
                order = list(BANKS)
                n, back = order.index(group), 0
                while back <= 3:
                    n -= 1
                    if n < 0:
                        n, back = len(order) - 1, back + 1
                    if BANKS[order[n]] == BANKS[group]:
                        other = chunk + BANK_LEAD[order[n]] - BANK_LEAD[group] - back
                        if not isinstance(other, int) or 0 <= other < CHUNKS:
                            ms, step = READ_BY[order[n]]
                            pe.wait_ge(ms.sem(step), ms.after(step, other))
                            return

            def transposes(ms, group, src, chunk):
                bank_free(group, chunk)
                for t in range(T):
                    last = nc.tensor.transpose(bank(group)[:, t * P:(t + 1) * P], src(t), ident[:, :])
                last.then_inc(ms.sem(group), ms.step(group))

            def n_transpose(a):
                pe.wait_ge(head_pool.sem("nf"), head_pool.after("nf", a))
                transposes(attn_tensor, "nT", lambda t: NF[:, t, :], a)

            def m_transpose(a):
                pe.wait_ge(attn_vector.sem("m"), attn_vector.after("m", a))
                transposes(attn_tensor, "mT", lambda t: X1[:, t, :], a)

            def out_transpose(a):
                pe.wait_ge(attn_scalar.sem("fm_out"), attn_scalar.after("fm_out", a))
                transposes(attn_tensor, "oT", lambda t: OTA[:, t * P:(t + 1) * P], a)

            def y_transpose(f):
                pe.wait_ge(ffn_vector.sem("y"), ffn_vector.after("y", f))
                transposes(ffn_tensor, "yT", lambda t: YF[:, t, :], f)

            def end_transpose(e):
                pe.wait_ge(ffn_scalar.sem("w3"), ffn_scalar.after("w3", e))
                transposes(end_tensor, "fT", lambda t: OTF[:, t * P:(t + 1) * P], e)

            def up(L, j, a):
                g = f"{L}u{j}"
                bank_free(g, a)
                if L != "h2" and j == 0 and isinstance(a, int) and a == 0:
                    pe.wait_ge(split_lo_a, 3 if L == "fm" else 1)
                    if L == "fm":
                        pe.wait_ge(lo_flagged, 1)
                if j == 0:
                    pe.wait_ge(attn_scalar.sem("mT_hi" if L == "fm" else "nT_hi"), attn_scalar.after("mT_hi" if L == "fm" else "nT_hi", a))
                xT = mT if L == "fm" else aT
                w = slice(A_UP[L] + j * P, A_UP[L] + (j + 1) * P)
                nc.tensor.matmul(bank(g)[:, :], Aw[1][:, w], xT[0][:, :], start=True, stop=False)
                nc.tensor.matmul(bank(g)[:, :], Aw[0][:, w], xT[0][:, :], start=False, stop=False)
                if j == 0:
                    pe.wait_ge(attn_vector.sem("mT_lo" if L == "fm" else "nT_lo"), attn_vector.after("mT_lo" if L == "fm" else "nT_lo", a))
                nc.tensor.matmul(bank(g)[:, :], Aw[0][:, w], xT[1][:, :], start=False, stop=True)\
                    .then_inc(attn_tensor.sem(g), attn_tensor.step(g))

            def down(L, k, a):
                g = f"{L}d"
                if k == 0:
                    bank_free(g, a)
                    if L == "h1" and isinstance(a, int) and a == 0:
                        pe.wait_ge(split_lo_a, 2)
                w = slice(A_DOWN[L] + k * P, A_DOWN[L] + (k + 1) * P)
                slot = (SLOT0[L] + k) % SLOTS
                pe.wait_ge(attn_scalar.sem(f"{L}_hi{k}"), attn_scalar.after(f"{L}_hi{k}", a))
                nc.tensor.matmul(bank(g)[:, :], Aw[1][:, w], HA[0][:, slot, :], start=(k == 0), stop=False)
                nc.tensor.matmul(bank(g)[:, :], Aw[0][:, w], HA[0][:, slot, :], start=False, stop=False)
                pe.wait_ge(attn_vector.sem(f"{L}_lo{k}"), attn_vector.after(f"{L}_lo{k}", a))
                last = nc.tensor.matmul(bank(g)[:, :], Aw[0][:, w], HA[1][:, slot, :], start=False, stop=(k == J - 1))
                if k == J - 1:
                    last.then_inc(attn_tensor.sem(g), attn_tensor.step(g))

            def scores(b, a):
                g = f"s{b}"
                bank_free(g, a)
                if b == 0:
                    pe.wait_ge(attn_vector.sem("h2T_lo"), attn_vector.after("h2T_lo", a))
                o = b * S
                W1, W2 = WT["h1"], WT["h2"]
                for c0, s0, z0, z1 in ((0, o, o, o + S), (2 * P, o + P, o + P, o + S)):
                    for n, (x2, x1) in enumerate(((1, 0), (0, 0), (0, 1))):
                        last = nc.tensor.matmul(bank(g)[:, c0:c0 + z1 - z0], W2[x2][:, s0:s0 + P], W1[x1][:, z0:z1],
                                                start=(n == 0), stop=(n == 2))
                last.then_inc(attn_tensor.sem(g), attn_tensor.step(g))

            def t_product(a):
                bank_free("t", a)
                pe.wait_ge(head_pool.sem("n_lo"), head_pool.after("n_lo", a))
                for b in range(SEQS):
                    pe.wait_ge(attn_vector.sem(f"s_lo{b}"), attn_vector.after(f"s_lo{b}", a))
                    for z, blocks in ((0, ((0, 0),)), (1, ((1, 0), (2, 1)))):
                        c0 = (2 * b + z) * P
                        steps = [(k, s, i, j) for k, s in blocks for i, j in ((1, 0), (0, 0), (0, 1))]
                        for n, (k, s, i, j) in enumerate(steps):
                            last = nc.tensor.matmul(bank("t")[:, c0:c0 + P], SC[i][:, b, k, :], n_tok[j][:, 2 * b + s, :],
                                                    start=(n == 0), stop=(n == len(steps) - 1))
                last.then_inc(attn_tensor.sem("t"), attn_tensor.step("t"))

            def gate(x, j, lo_pass, f):
                g = f"{x}{j}"
                bank_free(g, f)
                base = {"p": F_W1, "q": F_W2}[x]
                w = slice(base + j * P, base + (j + 1) * P)
                if g == "p0":
                    pe.wait_ge(ffn_scalar.sem("yT_hi"), ffn_scalar.after("yT_hi", f))
                if lo_pass:
                    nc.tensor.matmul(bank(g)[:, :], Fw[1][:, w], yT[0][:, :], start=True, stop=False)
                nc.tensor.matmul(bank(g)[:, :], Fw[0][:, w], yT[0][:, :], start=not lo_pass, stop=False)
                if g == "p0":
                    pe.wait_ge(ffn_vector.sem("yT_lo"), ffn_vector.after("yT_lo", f))
                nc.tensor.matmul(bank(g)[:, :], Fw[0][:, w], yT[1][:, :], start=False, stop=True)\
                    .then_inc(ffn_tensor.sem(g), ffn_tensor.step(g))

            def layer(L, j, lo_pass, f):
                g = {"h1": f"h1_{j}", "h2": f"h2_{j}", "w3": "w3"}[L]
                src, base, width, of = {"h1": (HG, F_H1, DI, "g"), "h2": (HF, F_H2, DI, "h1"), "w3": (HG, F_W3, P, "h2")}[L]
                bank_free(g, f)
                order = [(half, k) for half in (0, 1) for k in range(J)] if j == 0 else \
                    [(half, k) for k in range(J) for half in (0, 1)]
                for n, (half, k) in enumerate(order):
                    if j == 0:
                        ms, name = ((ffn_vector, f"{of}_lo{k}") if half else (ffn_scalar, f"{of}_hi{k}"))
                        pe.wait_ge(ms.sem(name), ms.after(name, f))
                    w = slice(base + k * width + j * P, base + k * width + (j + 1) * P)
                    if lo_pass and not half:
                        nc.tensor.matmul(bank(g)[:, :], Fw[1][:, w], src[0][:, k, :], start=(n == 0), stop=False)
                    last = nc.tensor.matmul(bank(g)[:, :], Fw[0][:, w], src[half][:, k, :],
                                            start=(n == 0 and not lo_pass), stop=(n == 2 * J - 1))
                last.then_inc(ffn_tensor.sem(g), ffn_tensor.step(g))

            def count_low_parts():
                bank_free("fmu0", 0)
                pe.wait_ge(lo_tested, 1)
                nc.tensor.matmul(bank("fmu0")[0:1, 0:4], ones[:, :], lo_any[:, :], start=True, stop=True).then_inc(lo_counted, 1)

            def iteration(i, lo_pass):
                on(i, y_transpose)
                on(i + 1, up, "h2", 3)
                on(i - 1, end_transpose)
                on(i + 1, down, "h2", 1)
                on(i, gate, "p", 0, lo_pass)
                on(i, gate, "q", 0, lo_pass)
                on(i + 1, down, "h2", 2)
                on(i + 1, down, "h2", 3)
                on(i, gate, "p", 1, lo_pass)
                on(i, gate, "q", 1, lo_pass)
                on(i, gate, "q", 2, lo_pass)
                on(i, gate, "p", 2, lo_pass)
                on(i + 1, scores, 0)
                on(i + 1, scores, 1)
                on(i, gate, "p", 3, lo_pass)
                on(i, gate, "q", 3, lo_pass)
                on(i + 2, n_transpose)
                on(i + 1, t_product)
                on(i + 2, up, "h1", 0)
                on(i + 2, up, "h1", 1)
                on(i, layer, "h1", 0, lo_pass)
                on(i, layer, "h1", 1, lo_pass)
                on(i, layer, "h1", 2, lo_pass)
                on(i, layer, "h1", 3, lo_pass)
                on(i + 1, m_transpose)
                once(i + 1, count_low_parts)
                on(i, layer, "h2", 0, lo_pass)
                on(i + 1, up, "fm", 0)
                on(i + 1, up, "fm", 1)
                on(i + 1, up, "fm", 2)
                on(i, layer, "h2", 1, lo_pass)
                on(i + 1, up, "fm", 3)
                on(i + 1, down, "fm", 0)
                on(i + 1, down, "fm", 1)
                on(i + 2, up, "h1", 2)
                on(i + 1, down, "fm", 2)
                on(i + 1, down, "fm", 3)
                on(i + 2, down, "h1", 0)
                on(i + 1, out_transpose)
                on(i + 2, up, "h2", 0)
                on(i + 2, up, "h1", 3)
                on(i, layer, "h2", 2, lo_pass)
                on(i + 2, down, "h1", 1)
                on(i, layer, "h2", 3, lo_pass)
                on(i + 2, up, "h2", 1)
                on(i + 2, down, "h1", 2)
                on(i + 2, down, "h1", 3)
                on(i + 2, up, "h2", 2)
                on(i, layer, "w3", 0, lo_pass)
                on(i + 2, down, "h2", 0)

            pe.wait_ge(consts_ready, 4)
            for i in range(-LEADS["tensor"][1], 0):
                iteration(i, False)
            pe.wait_ge(split_lo_f, 4)
            pe.wait_ge(lo_flagged, 1)
            any_lo = pe.value_load(lo_flag[0:1, 0:1].bitcast(i32))

            def stream(lo_pass):
                iterations(pe, lambda i: iteration(i, lo_pass), LEADS["tensor"], first=0)

            with pe.If(any_lo > 0):
                stream(True)
            with pe.Else():
                stream(False)


def kernel(**inputs):
    import numpy as _np
    import concourse.bacc as _bacc
    from concourse import mybir as _mybir
    from concourse.bass_utils import run_bass_kernel_spmd as _run

    g = {k: _np.asarray(v) for k, v in inputs.items()}

    def k_tiles(w):
        return w.reshape(-1, 128, w.shape[1]).transpose(1, 0, 2).reshape(128, -1)

    def by_partition(v):
        return v.reshape(-1, 128).T

    a, f = "L0_attn_", "L0_ffn_"
    arrays = {
        "x": g[a + "x"],
        "attn_w": _np.concatenate([g[a + "h1_w1"], g[a + "h2_w1"], k_tiles(g[a + "h1_w2"]), k_tiles(g[a + "h2_w2"]),
                                   g[a + "fm_w1"], k_tiles(g[a + "fm_w2"])], axis=1),
        "ffn_w": _np.concatenate([k_tiles(g[f + n].T) for n in ("w1_w", "w2_w", "w3_w", "h1_w", "h2_w")], axis=1),
        "columns": _np.concatenate([by_partition(g[n]) for n in (
            a + "h1_b1", a + "h2_b1", a + "fm_b1", f + "w1_s", f + "w2_s", f + "h1_s", f + "h2_s",
            a + "h1_b2", a + "h2_b2", a + "ln_g", a + "ln_b", f + "w3_s")], axis=1),
        "rows": _np.stack([g[a + "ln_g"], g[a + "ln_b"], g[a + "fm_b2"]]),
    }
    nc = _bacc.Bacc("TRN2", target_bir_lowering=False, num_devices=1)
    args = []
    for name in arrays:
        arrays[name] = _np.ascontiguousarray(arrays[name])
        args.append(nc.dram_tensor(name, arrays[name].shape, _mybir.dt.from_np(arrays[name].dtype), kind="ExternalInput").ap())
    out = nc.dram_tensor("out", g[a + "x"].shape, _mybir.dt.from_np(g[a + "x"].dtype), kind="ExternalOutput").ap()
    sandwich_block(nc, *args, out)
    r = _run(nc, [arrays], core_ids=[0])
    return r.results[0]["out"]
```
